# Optimizing a Trainium2 kernel written in Bass

```python
import numpy as np
import jax
import jax.numpy as jnp

def _softmax(x, axis=-1):
    return jax.nn.softmax(x, axis=axis)

def _gelu(x):
    return jax.nn.gelu(x, approximate=True)

def _silu(x):
    return jax.nn.silu(x)

def _sigmoid(x):
    return jax.nn.sigmoid(x)

def _layernorm(x, axis=-1, eps=1e-05):
    m = jnp.mean(x, axis=axis, keepdims=True)
    v = jnp.var(x, axis=axis, keepdims=True)
    return (x - m) / jnp.sqrt(v + eps)

def _scatter_add(tgt, idx, src, axis=0):
    return tgt.at[idx].add(src)

def _segment_sum(src, seg, n):
    return jax.ops.segment_sum(src, seg, n)
kernel_name = 'mk_adj_preln_d1_adj_r2_fc8ceb'

def setup_inputs(seed: int=0):
    np.random.seed(seed)
    _w = jnp.asarray

    def _rec_inputs():
        import jax
        import jax.numpy as jnp
        _gk = jax.random.key(seed)
        x = -0.0002928 + 1 * jax.random.normal(jax.random.fold_in(_gk, 1), (4096, 256), jnp.float32)
        _a = jax.random.bernoulli(jax.random.fold_in(_gk, 2), 0.00390625, (4096, 4096))
        adj = _a
        return (x, adj)
    x, adj = _rec_inputs()

    def _L0_gnn_setup():
        import jax, jax.numpy as jnp
        import numpy as np
        N = 4096
        D = 256
        NEG = -1e+30
        key = jax.random.key(seed)
        ks = jax.random.split(key, 5)
        neuron_states = jax.random.normal(ks[0], (N, D), dtype=jnp.float32)
        adjacency = jax.random.bernoulli(ks[1], 0.05, (N, N))
        Wq = jax.random.normal(ks[2], (D, D), dtype=jnp.float32) / np.sqrt(D)
        Wk = jax.random.normal(ks[3], (D, D), dtype=jnp.float32) / np.sqrt(D)
        Wv = jax.random.normal(ks[4], (D, D), dtype=jnp.float32) / np.sqrt(D)
        return {'neuron_states': neuron_states, 'adjacency': adjacency, 'Wq': Wq, 'Wk': Wk, 'Wv': Wv}
    _L0_gnn_all = _L0_gnn_setup()
    _L0_gnn_in = {k: v for k, v in _L0_gnn_all.items() if k in ('Wq', 'Wk', 'Wv')}
    del _L0_gnn_all
    return {'x': x, 'adj': adj, 'L0_gnn_Wq': _L0_gnn_in['Wq'], 'L0_gnn_Wk': _L0_gnn_in['Wk'], 'L0_gnn_Wv': _L0_gnn_in['Wv']}

def reference(x, adj, L0_gnn_Wq, L0_gnn_Wk, L0_gnn_Wv):
    import jax
    import jax.numpy as jnp

    def _L0_gnn_ref(neuron_states, adjacency, Wq, Wk, Wv):
        import jax, jax.numpy as jnp
        import numpy as np
        N = 4096
        D = 256
        NEG = -1e+30
        q = neuron_states @ Wq.T
        k = neuron_states @ Wk.T
        v = neuron_states @ Wv.T
        mask = adjacency.T
        scores = jnp.where(mask, q @ k.T, NEG)
        attn = jax.nn.softmax(scores, axis=1)
        attn = jnp.where(mask, attn, 0.0)
        return attn @ v
    h = jnp.maximum(_layernorm(x, axis=-1), 0.0)
    x = x + _L0_gnn_ref(h, adj, L0_gnn_Wq, L0_gnn_Wk, L0_gnn_Wv)
    return x

_drawn_inputs = setup_inputs


def setup_inputs(seed=0):
    import zlib

    import numpy as np

    out = dict(_drawn_inputs(seed))
    spreads = {}
    factors = {}
    for name, (base, spread) in spreads.items():
        noise = np.random.default_rng([zlib.crc32(name.encode()), seed]).standard_normal(out[name].shape)
        drawn = base * np.exp(spread * noise) if base else spread * noise
        out[name] = jnp.asarray(drawn.astype(out[name].dtype))
    for name, factor in factors.items():
        out[name] = (out[name] * factor).astype(out[name].dtype)
    return out
```

```python
import math
from contextlib import ExitStack

import concourse.bass as bass
from concourse import mybir

ALU = mybir.AluOpType
ACT = mybir.ActivationFunctionType
AX_X = mybir.AxisListType.X
F32 = mybir.dt.float32
F16 = mybir.dt.float16
U8 = mybir.dt.uint8

P = 128
LN_EPS = 1e-5
MASKED = -1e30
NO_EDGE_MAX = -1e29
OPERAND_SCALE = 1024.0
SQUARES_FLOOR = 1e-30
LOG_P_SCALE = 14 * math.log(2.0)


def attention_layer(nc, x, adj, Wq, Wk, Wv, out):
    N, D = x.shape
    KC = D // P
    CHUNKS = N // P
    Q = 256
    QT = Q // P
    BLOCKS = N // Q
    BANK = 512
    SEG_CHUNKS = 4
    SEGS = CHUNKS // SEG_CHUNKS
    GROUPS = 4
    GC = CHUNKS // GROUPS
    XG = 4
    XGROUPS = CHUNKS // XG
    assert KC == 2 and QT == 2 and GC == 2 * SEG_CHUNKS and XG * P == BANK and Q == D

    x_chunks = x.rearrange("(c p) d -> p c d", p=P)
    adj_chunks = adj.rearrange("(c p) i -> p c i", p=P)

    with ExitStack() as ctx:
        def sb(name, shape, dt):
            return ctx.enter_context(nc.sbuf_tensor(name, shape, dt))

        def ps(name, shape):
            return ctx.enter_context(nc.psum_tensor(name, shape, F32))

        def sem(name):
            return ctx.enter_context(nc.semaphore(name))

        hT_hi = sb("hT_hi", [P, KC, N], F16)
        hT_lo = sb("hT_lo", [P, KC, N], F16)
        v_hi = sb("v_hi", [P, CHUNKS, D + 2], F16)
        v_lo = sb("v_lo", [P, CHUNKS, D], F16)
        gT_hi = sb("gT_hi", [P, KC, Q], F16)
        gT_lo = sb("gT_lo", [P, KC, Q], F16)
        score = [sb(f"score{i}", [P, CHUNKS, Q], F32) for i in range(2)]
        x_in = score[1]
        p_hi = sb("p_hi", [P, CHUNKS, Q], F16)
        p_lo = sb("p_lo", [P, CHUNKS, Q], F16)
        edges = [sb(f"edges{i}", [P, CHUNKS, Q], U8) for i in range(2)]
        wq, wk, wv = (p_hi[:, 4 * i:4 * (i + 1), :].rearrange("p c q -> p (c q)").bitcast(F32)
                      .rearrange("p (k d) -> p k d", k=KC) for i in range(3))
        a_f, squares = (p_hi[:, 4 * i:4 * (i + 1), :].rearrange("p c q -> p (c q)").bitcast(F32) for i in (3, 4))
        a_hi = sb("a_hi", [P, KC, D], F16)
        a_lo = sb("a_lo", [P, KC, D], F16)
        wvT_hi = sb("wvT_hi", [P, KC, D], F16)
        wvT_lo = sb("wvT_lo", [P, KC, D], F16)
        ident = sb("ident", [P, P], F32)
        ones = sb("ones", [P, P], F32)
        norm_diag = sb("norm_diag", [P, KC, P], F32)
        v_scale_row = sb("v_scale_row", [P, D], F32)
        sumsq = sb("sumsq", [P, 3], F32)
        norm = sb("norm", [P, 3], F32)
        inv_norm = sb("inv_norm", [P, 3], F32)
        score_scale = sb("score_scale", [P, 1], F32)
        log_p_scale = sb("log_p_scale", [P, 1], F32)
        stats = sb("stats", [P, CHUNKS, 6], F32)
        mean_var = sb("mean_var", [P, CHUNKS, 2], F32)
        var_eps = sb("var_eps", [P, CHUNKS], F32)
        std = sb("std", [P, CHUNKS], F32)
        rstd0 = sb("rstd0", [P, CHUNKS], F32)
        newton = sb("newton", [P, CHUNKS], F32)
        rstd = sb("rstd", [P, CHUNKS], F32)
        group_max = sb("group_max", [P, GROUPS, Q], F32)
        block_max = sb("block_max", [P, Q], F32)
        query_max = sb("query_max", [P, QT], F32)
        max_diag = sb("max_diag", [P, QT, P], F32)
        max_row = sb("max_row", [P, Q], F32)
        sums = sb("sums", [P, QT], F32)
        inv_sums = sb("inv_sums", [P, QT], F32)
        attn = sb("attn", [P, QT, D], F32)
        x_res = sb("x_res", [P, QT, D], F32)
        y = sb("y", [P, QT, D], F32)

        seg_ps = [ps(f"seg_ps{i}", [P, 2 * BANK]) for i in range(2)]
        acc_ps = [ps(f"acc_ps{i}", [P, BANK]) for i in range(QT)]
        g_ps = ps("g_ps", [P, KC * Q])
        max_ps = ps("max_ps", [P, BANK])
        w_ps, aux_ps = g_ps, max_ps

        x_loaded = [sem(f"x_loaded{g}") for g in range(XGROUPS)]
        weights_loaded = sem("weights_loaded")
        edges_loaded = sem("edges_loaded")
        x_res_loaded = sem("x_res_loaded")
        y_stored = sem("y_stored")
        zeroed = sem("zeroed")
        consts_ready = sem("consts_ready")
        product_ready = sem("product_ready")
        squares_ready = sem("squares_ready")
        total_ready = sem("total_ready")
        norms_ready = sem("norms_ready")
        wv_scaled = sem("wv_scaled")
        wvT_ready = sem("wvT_ready")
        wvT_hi_ready = sem("wvT_hi_ready")
        weights_split = sem("weights_split")
        a_hi_ready = sem("a_hi_ready")
        var_ready = sem("var_ready")
        std_ready = sem("std_ready")
        xn_ready = sem("xn_ready")
        xT_ready = sem("xT_ready")
        hT_hi_ready = sem("hT_hi_ready")
        hT_ready = sem("hT_ready")
        v_ps_ready = sem("v_ps_ready")
        v_hi_ready = sem("v_hi_ready")
        v_ready = sem("v_ready")
        g_ps_ready = sem("g_ps_ready")
        g_hi_ready = sem("g_hi_ready")
        g_ready = sem("g_ready")
        block_max_ready = sem("block_max_ready")
        max_turned = sem("max_turned")
        max_diag_ready = sem("max_diag_ready")
        max_row_ps_ready = sem("max_row_ps_ready")
        max_row_ready = sem("max_row_ready")
        attn_ready = sem("attn_ready")
        y_ready = sem("y_ready")
        scores_ready = sem("scores_ready")
        scores_masked = sem("scores_masked")
        filled = sem("filled")
        shifted = sem("shifted")
        exp_ready = sem("exp_ready")
        hi_ready = sem("hi_ready")
        lo_ready = sem("lo_ready")
        weighted = sem("weighted")
        dve_step = sem("dve_step")

        def wait_reuse(engine, semaphore, value):
            if not isinstance(value, int) or value > 0:
                engine.wait_ge(semaphore, value)

        def wait_alone(engine, semaphore, value):
            wait_reuse(engine, semaphore, value)
            engine.nop(nofuse=True)

        LOOP_FROM, LOOP_TO = 4, BLOCKS - 2

        def stages(engine, stage):
            for i in range(LOOP_FROM):
                stage(i, i % 2)
            with engine.Fori(LOOP_FROM, LOOP_TO, 2) as i:
                stage(i, 0)
                stage(i + 1, 1)
            for i in range(LOOP_TO, BLOCKS + 2):
                stage(i, i % 2)

        def exists(block):
            return not isinstance(block, int) or 0 <= block < BLOCKS

        block = ctx.enter_context(nc.Block())

        @block.sync
        def _(sp):
            def load_x(g):
                sp.dma_start(x_in[:, g * XG:(g + 1) * XG, :],
                             x_chunks[:, g * XG:(g + 1) * XG, :]).then_inc(x_loaded[g], 16)

            load_x(0)
            load_x(1)
            for w_sb, w in ((wq, Wq), (wk, Wk), (wv, Wv)):
                sp.dma_start(w_sb[:, :, :], w.rearrange("(c p) d -> p c d", p=P)).then_inc(weights_loaded, 16)
            for g in range(2, XGROUPS):
                load_x(g)

            def load_edges(b, par):
                wait_alone(sp, edges_loaded, 16 * b)
                wait_alone(sp, scores_masked, SEGS * (b - 1))
                sp.dma_start(edges[par][:, :, :], adj_chunks[:, :, bass.ds(b * Q, Q)]).then_inc(edges_loaded, 16)

            def rows(t, b):
                return t[bass.ds(b * Q, Q), :].rearrange("(t p) d -> p t d", p=P)

            def load_residual(b):
                wait_alone(sp, y_ready, b)
                sp.dma_start(x_res[:, :, :], rows(x, b)).then_inc(x_res_loaded, 16)

            def store(b):
                wait_alone(sp, y_ready, b + 1)
                sp.dma_start(rows(out, b), y[:, :, :]).then_inc(y_stored, 16)

            def stage(i, par):
                if exists(i + 1):
                    load_edges(i + 1, 1 - par)
                if exists(i - 2):
                    load_residual(i - 2)
                    store(i - 2)

            load_edges(0, 0)
            stages(sp, stage)
            sp.wait_ge(y_stored, 16 * BLOCKS)

        @block.gpsimd
        def _(pool):
            pool.memset(ident[:, :], 0.0).then_inc(zeroed, 1)
            pool.memset(ones[:, :], 1.0)
            pool.memset(v_hi[:, :, D:D + 2], 1.0)
            pool.memset(log_p_scale[:, :], LOG_P_SCALE)
            pool.wait_ge(zeroed, 1)
            pool.affine_select(out=ident[:, :], in_=ident[:, :], compare_op=ALU.not_equal, fill=1.0,
                               base=0, pattern=[[-1, P]], channel_multiplier=1).then_inc(consts_ready, 1)

            def fill(par, g):
                pool.memset(score[par][:, g * GC:(g + 1) * GC, :], MASKED).then_inc(filled, 1)

            def shift(b, par, g):
                if g == 0:
                    pool.wait_ge(max_row_ready, b + 1)
                group = score[par][:, g * GC:(g + 1) * GC, :]
                pool.tensor_tensor(group, group, max_row[:, None, :].to_broadcast([P, GC, Q]),
                                   ALU.subtract).then_inc(shifted, 1)

            def finish(b):
                pool.wait_ge(attn_ready, b + 1)
                pool.wait_ge(x_res_loaded, 16 * b + 16)
                wait_reuse(pool, y_stored, 16 * b)
                pool.tensor_tensor(y[:, :, :], attn[:, :, :], x_res[:, :, :], ALU.add).then_inc(y_ready, 1)

            def stage(i, par):
                if exists(i - 1):
                    for g in range(GROUPS):
                        shift(i - 1, 1 - par, g)
                for g in range(GROUPS):
                    if g == GROUPS - 1 and exists(i - 2):
                        finish(i - 2)
                    if exists(i + 1):
                        if isinstance(i, int) and i == 0:
                            pool.wait_ge(xT_ready, XGROUPS)
                        else:
                            wait_alone(pool, lo_ready, GROUPS * (i - 1) + g + 1)
                        fill(1 - par, g)

            for g in range(GROUPS):
                fill(0, g)
            stages(pool, stage)

        @block.scalar
        def _(act):
            def group_std(g):
                act.wait_ge(var_ready, g + 1)
                cols = slice(g * XG, (g + 1) * XG)
                act.activation(std[:, cols], var_eps[:, cols], ACT.Sqrt).then_inc(std_ready, 1)

            def group_hT_hi(g):
                act.wait_ge(xT_ready, g + 1)
                for k in range(KC):
                    last = act.activation(hT_hi[:, k, g * BANK:(g + 1) * BANK],
                                          seg_ps[g % 2][:, k * BANK:(k + 1) * BANK], ACT.Relu)
                last.then_inc(hT_hi_ready, 1)

            act.wait_ge(weights_loaded, 48)
            for k in range(KC):
                last = act.activation(squares[:, k * D:(k + 1) * D], wv[:, k, :], ACT.Square,
                                      accum_out=sumsq[:, 1 + k:2 + k])
            last.then_inc(squares_ready, 1)
            act.wait_ge(product_ready, 1)
            act.wait_ge(squares_ready, 1)
            act.activation(squares[:, :], w_ps[:, :], ACT.Square,
                           accum_out=sumsq[:, 0:1]).then_inc(squares_ready, 1)
            act.wait_ge(total_ready, 1)
            act.activation(norm[:, :], inv_norm[:, :], ACT.Sqrt).then_inc(norms_ready, 1)
            act.wait_ge(total_ready, 2)
            act.activation(a_hi[:, :, :].rearrange("p k d -> p (k d)"), a_f[:, :], ACT.Copy).then_inc(a_hi_ready, 1)
            act.wait_ge(wvT_ready, 1)
            act.activation(wvT_hi[:, :, :].rearrange("p k d -> p (k d)"), w_ps[:, :], ACT.Copy).then_inc(wvT_hi_ready, 1)
            for g in range(XGROUPS + 1):
                if g < XGROUPS:
                    group_std(g)
                if g >= 1:
                    group_hT_hi(g - 1)

            def split_g_hi(b):
                act.wait_ge(g_ps_ready, b + 1)
                wait_reuse(act, scores_ready, SEGS * b)
                act.activation(gT_hi[:, :, :].rearrange("p k d -> p (k d)"), g_ps[:, :], ACT.Copy
                               ).then_inc(g_hi_ready, 1)

            def take_max_row(b):
                act.wait_ge(max_row_ps_ready, b + 1)
                wait_reuse(act, shifted, GROUPS * b)
                act.activation(max_row[:, :], max_ps[:, Q:2 * Q], ACT.Copy).then_inc(max_row_ready, 1)

            def exponentials(b, par, g):
                act.wait_ge(shifted, GROUPS * b + g + 1)
                group = score[par][:, g * GC:(g + 1) * GC, :].rearrange("p c q -> p (c q)")
                act.activation(group, group, ACT.Exp, bias=log_p_scale[:, 0:1],
                               scale=score_scale[:, 0:1]).then_inc(exp_ready, 1)

            def split_p_hi(b, par, g):
                act.wait_ge(exp_ready, GROUPS * b + g + 1)
                wait_reuse(act, weighted, GROUPS * (b - 1) + g + 1)
                act.activation(p_hi[:, g * GC:(g + 1) * GC, :].rearrange("p c q -> p (c q)"),
                               score[par][:, g * GC:(g + 1) * GC, :].rearrange("p c q -> p (c q)"),
                               ACT.Copy).then_inc(hi_ready, 1)

            def v_hi_of(g):
                act.wait_ge(v_ps_ready, g + 1)
                act.activation(v_hi[:, g * XG:(g + 1) * XG, 0:D],
                               seg_ps[g % 2][:, :].rearrange("p (c d) -> p c d", d=D), ACT.Copy
                               ).then_inc(v_hi_ready, 1)

            def stage(i, par):
                if exists(i - 1):
                    take_max_row(i - 1)
                for g in range(GROUPS):
                    if exists(i - 1):
                        exponentials(i - 1, 1 - par, g)
                    if g == GROUPS - 1 and exists(i + 1):
                        split_g_hi(i + 1)
                    if exists(i - 1):
                        split_p_hi(i - 1, 1 - par, g)
                if isinstance(i, int) and i == 0:
                    for g in range(XGROUPS):
                        v_hi_of(g)

            split_g_hi(0)
            stages(act, stage)

        @block.vector
        def _(dve):
            steps = [0]

            def step(instruction):
                instruction.then_inc(dve_step, 1)
                steps[0] = steps[0] + 1
                dve.wait_ge(dve_step, steps[0])

            def group_stats(g):
                dve.wait_ge(x_loaded[g], 16)
                for c in range(g * XG, (g + 1) * XG):
                    last = dve.bn_stats(stats[:, c, :], x_in[:, c, :])
                step(last)
                for c in range(g * XG, (g + 1) * XG):
                    last = dve.bn_aggr(mean_var[:, c, :], stats[:, c, :])
                step(last)
                dve.tensor_scalar(var_eps[:, g * XG:(g + 1) * XG],
                                  mean_var[:, g * XG:(g + 1) * XG, 1], LN_EPS, None,
                                  ALU.add).then_inc(var_ready, 1)

            def group_normalise(g):
                cols = slice(g * XG, (g + 1) * XG)
                dve.wait_ge(std_ready, g + 1)
                step(dve.reciprocal(rstd0[:, cols], std[:, cols]))
                step(dve.tensor_tensor(newton[:, cols], rstd0[:, cols], rstd0[:, cols], ALU.mult))
                step(dve.tensor_tensor(newton[:, cols], newton[:, cols], var_eps[:, cols], ALU.mult))
                step(dve.tensor_scalar(newton[:, cols], newton[:, cols], -0.5, 1.5, ALU.mult, ALU.add))
                step(dve.tensor_tensor(rstd[:, cols], newton[:, cols], rstd0[:, cols], ALU.mult))
                for c in range(g * XG, (g + 1) * XG):
                    last = dve.tensor_scalar(x_in[:, c, :], x_in[:, c, :], mean_var[:, c, 0:1],
                                             rstd[:, c:c + 1], ALU.subtract, ALU.mult)
                last.then_inc(xn_ready, 1)

            def group_hT_lo(g):
                dve.wait_ge(hT_hi_ready, g + 1)
                for k in range(KC):
                    cols = slice(g * BANK, (g + 1) * BANK)
                    last = dve.scalar_tensor_tensor(hT_lo[:, k, cols], seg_ps[g % 2][:, k * BANK:(k + 1) * BANK],
                                                    0.0, hT_hi[:, k, cols], ALU.max, ALU.subtract)
                last.then_inc(hT_ready, 1)

            def split_weights():
                dve.wait_ge(squares_ready, 2)
                dve.wait_ge(product_ready, 2)
                dve.tensor_scalar(inv_norm[:, 0:1], aux_ps[:, 0:1], SQUARES_FLOOR, None, ALU.max)
                dve.tensor_scalar(inv_norm[:, 1:3], sumsq[:, 1:3], SQUARES_FLOOR, None,
                                  ALU.max).then_inc(total_ready, 1)
                dve.wait_ge(norms_ready, 1)
                step(dve.reciprocal(inv_norm[:, :], norm[:, :]))
                dve.tensor_scalar(a_f[:, :], w_ps[:, :], inv_norm[:, 0:1], OPERAND_SCALE,
                                  ALU.mult, ALU.mult).then_inc(total_ready, 1)
                dve.tensor_scalar(score_scale[:, :], norm[:, 0:1], 1.0 / OPERAND_SCALE, None, ALU.mult)
                for k in range(KC):
                    dve.tensor_scalar(wv[:, k, :], wv[:, k, :], inv_norm[:, 1 + k:2 + k], OPERAND_SCALE,
                                      ALU.mult, ALU.mult)
                    last = dve.tensor_scalar(norm_diag[:, k, :], ident[:, :], norm[:, 1 + k:2 + k],
                                             1.0 / OPERAND_SCALE, ALU.mult, ALU.mult)
                last.then_inc(wv_scaled, 1)
                dve.wait_ge(a_hi_ready, 1)
                dve.tensor_tensor(a_lo[:, :, :].rearrange("p k d -> p (k d)"), a_f[:, :],
                                  a_hi[:, :, :].rearrange("p k d -> p (k d)"), ALU.subtract)
                dve.wait_ge(wvT_hi_ready, 1)
                dve.tensor_tensor(wvT_lo[:, :, :].rearrange("p k d -> p (k d)"), w_ps[:, :],
                                  wvT_hi[:, :, :].rearrange("p k d -> p (k d)"), ALU.subtract)
                dve.wait_ge(product_ready, 3)
                dve.tensor_copy(v_scale_row[:, :], aux_ps[:, 0:D]).then_inc(weights_split, 1)

            dve.wait_ge(consts_ready, 1)
            split_weights()
            for g in range(XGROUPS + 2):
                if g < XGROUPS:
                    group_stats(g)
                if 1 <= g <= XGROUPS:
                    group_normalise(g - 1)
                if g >= 2:
                    group_hT_lo(g - 2)

            def split_g_lo(b):
                dve.wait_ge(g_hi_ready, b + 1)
                dve.tensor_tensor(gT_lo[:, :, :].rearrange("p k d -> p (k d)"), g_ps[:, :],
                                  gT_hi[:, :, :].rearrange("p k d -> p (k d)"), ALU.subtract).then_inc(g_ready, 1)

            def mask(b, par, s):
                if s == 0:
                    dve.wait_ge(edges_loaded, 16 * b + 16)
                if s % 2 == 0:
                    dve.wait_ge(filled, GROUPS * b + s // 2 + 1)
                wait_alone(dve, scores_ready, SEGS * b + s + 1)
                chunks = slice(s * SEG_CHUNKS, (s + 1) * SEG_CHUNKS)
                dve.copy_predicated(score[par][:, chunks, :].rearrange("p c q -> p (c q)"),
                                    edges[par][:, chunks, :].rearrange("p c q -> p (c q)"),
                                    seg_ps[s % 2][:, :]).then_inc(scores_masked, 1)

            def max_over_group(b, par, g):
                dve.wait_ge(scores_masked, SEGS * b + 2 * g + 2)
                step(dve.reduce_max(group_max[:, g, :],
                                    score[par][:, g * GC:(g + 1) * GC, :].rearrange("p c q -> p q c"), AX_X))

            def max_over_chunks():
                dve.reduce_max(block_max[:, :], group_max[:, :, :].rearrange("p g q -> p q g"),
                               AX_X).then_inc(block_max_ready, 1)

            def max_over_partitions(b):
                dve.wait_ge(max_turned, b + 1)
                step(dve.reduce_max(query_max[:, :], max_ps[:, 0:Q].rearrange("p (t k) -> p t k", t=QT), AX_X))
                step(dve.tensor_scalar(query_max[:, :], query_max[:, :], NO_EDGE_MAX, None, ALU.max))
                for t in range(QT):
                    last = dve.tensor_scalar(max_diag[:, t, :], ident[:, :], query_max[:, t:t + 1], None, ALU.mult)
                last.then_inc(max_diag_ready, 1)

            def split_p_lo(b, par, g):
                dve.wait_ge(hi_ready, GROUPS * b + g + 1)
                chunks = slice(g * GC, (g + 1) * GC)
                dve.tensor_tensor(p_lo[:, chunks, :], score[par][:, chunks, :], p_hi[:, chunks, :],
                                  ALU.subtract).then_inc(lo_ready, 1)

            def scale_sums(b):
                dve.wait_ge(weighted, GROUPS * (b + 1))
                for t in range(QT):
                    last = dve.tensor_scalar(sums[:, t:t + 1], acc_ps[t][:, D:D + 1], 1.0, None, ALU.max)
                step(last)
                step(dve.reciprocal(inv_sums[:, :], sums[:, :]))
                wait_reuse(dve, y_ready, b)
                for t in range(QT):
                    last = dve.scalar_tensor_tensor(attn[:, t, :], acc_ps[t][:, 0:D], inv_sums[:, t:t + 1],
                                                    v_scale_row[:, :], ALU.mult, ALU.mult)
                last.then_inc(attn_ready, 1)

            def v_lo_of(g):
                dve.wait_ge(v_hi_ready, g + 1)
                dve.tensor_tensor(v_lo[:, g * XG:(g + 1) * XG, :],
                                  seg_ps[g % 2][:, :].rearrange("p (c d) -> p c d", d=D),
                                  v_hi[:, g * XG:(g + 1) * XG, 0:D], ALU.subtract).then_inc(v_ready, 1)

            STAGE_STEPS = GROUPS + 2 + 2

            def stage(i, par):
                if not isinstance(i, int) and par == 0:
                    steps[0] = loop_base[0] + (i - LOOP_FROM) * STAGE_STEPS
                for g in range(GROUPS):
                    if exists(i):
                        mask(i, par, 2 * g)
                    if g == 0 and exists(i - 1):
                        max_over_partitions(i - 1)
                    if exists(i):
                        mask(i, par, 2 * g + 1)
                        max_over_group(i, par, g)
                    if g == GROUPS - 1:
                        if exists(i):
                            max_over_chunks()
                        if exists(i + 1):
                            split_g_lo(i + 1)
                        if exists(i - 2):
                            scale_sums(i - 2)
                    if exists(i - 1):
                        split_p_lo(i - 1, 1 - par, g)
                if isinstance(i, int) and i == 0:
                    for g in range(XGROUPS):
                        v_lo_of(g)
                if isinstance(i, int) and i == LOOP_FROM - 1:
                    loop_base[0] = steps[0]

            loop_base = [0]
            split_g_lo(0)
            for i in range(LOOP_FROM):
                stage(i, i % 2)
            with dve.Fori(LOOP_FROM, LOOP_TO, 2) as i:
                stage(i, 0)
                stage(i + 1, 1)
            steps[0] = loop_base[0] + (LOOP_TO - LOOP_FROM) * STAGE_STEPS
            for i in range(LOOP_TO, BLOCKS + 2):
                stage(i, i % 2)

        @block.tensor
        def _(pe):
            pe.wait_ge(weights_loaded, 48)
            for m in range(KC):
                for k in range(KC):
                    last = pe.matmul(w_ps[:, m * D:(m + 1) * D], wq[:, k, m * P:(m + 1) * P], wk[:, k, :],
                                     start=(k == 0), stop=(k == KC - 1))
            last.then_inc(product_ready, 1)
            pe.wait_ge(consts_ready, 1)
            pe.wait_ge(squares_ready, 2)
            pe.matmul(aux_ps[:, 0:1], ones[:, :], sumsq[:, 0:1], start=True, stop=True).then_inc(product_ready, 1)
            pe.wait_ge(wv_scaled, 1)
            pe.wait_ge(a_hi_ready, 1)
            for k in range(KC):
                for m in range(KC):
                    last = pe.transpose(w_ps[:, m * D + k * P:m * D + (k + 1) * P],
                                        wv[:, k, m * P:(m + 1) * P], ident[:, :])
            last.then_inc(wvT_ready, 1)
            for k in range(KC):
                last = pe.matmul(aux_ps[:, k * P:(k + 1) * P], ones[:, :], norm_diag[:, k, :],
                                 start=True, stop=True)
            last.then_inc(product_ready, 1)
            for g in range(XGROUPS):
                pe.wait_ge(xn_ready, g + 1)
                if g >= 2:
                    pe.wait_ge(hT_ready, g - 1)
                for c in range(XG):
                    for k in range(KC):
                        last = pe.transpose(seg_ps[g % 2][:, k * BANK + c * P:k * BANK + (c + 1) * P],
                                            x_in[:, g * XG + c, k * P:(k + 1) * P], ident[:, :])
                last.then_inc(xT_ready, 1)

            def project_g(b):
                passes = [(a, h, k) for a, h in ((a_hi, hT_hi), (a_hi, hT_lo), (a_lo, hT_hi)) for k in range(KC)]
                for m in range(KC):
                    for i, (a, h, k) in enumerate(passes):
                        last = pe.matmul(g_ps[:, m * Q:(m + 1) * Q], a[:, k, m * P:(m + 1) * P],
                                         h[:, k, bass.ds(b * Q, Q)],
                                         start=(i == 0), stop=(i == len(passes) - 1))
                last.then_inc(g_ps_ready, 1)

            def scores(b, g):
                passes = [(h, q, k) for h, q in ((hT_hi, gT_hi), (hT_hi, gT_lo), (hT_lo, gT_hi)) for k in range(KC)]
                for s in (2 * g, 2 * g + 1):
                    wait_reuse(pe, scores_masked, SEGS * b + s - 1)
                    for j in range(SEG_CHUNKS):
                        c = s * SEG_CHUNKS + j
                        for i, (h, q, k) in enumerate(passes):
                            last = pe.matmul(seg_ps[s % 2][:, j * Q:(j + 1) * Q], h[:, k, c * P:(c + 1) * P],
                                             q[:, k, :], start=(i == 0), stop=(i == len(passes) - 1))
                    last.then_inc(scores_ready, 1)

            def turn_max(b):
                pe.wait_ge(block_max_ready, b + 1)
                wait_reuse(pe, max_row_ready, b)
                for t in range(QT):
                    last = pe.transpose(max_ps[:, t * P:(t + 1) * P], block_max[:, t * P:(t + 1) * P], ident[:, :])
                last.then_inc(max_turned, 1)

            def spread_max(b):
                pe.wait_ge(max_diag_ready, b + 1)
                for t in range(QT):
                    last = pe.matmul(max_ps[:, Q + t * P:Q + (t + 1) * P], ones[:, :], max_diag[:, t, :],
                                     start=True, stop=True)
                last.then_inc(max_row_ps_ready, 1)

            def project_v(g):
                if g >= 2:
                    pe.wait_ge(v_ready, g - 1)
                else:
                    pe.wait_ge(scores_masked, SEGS)
                passes = [(h, w, k) for h, w in ((hT_hi, wvT_hi), (hT_hi, wvT_lo), (hT_lo, wvT_hi)) for k in range(KC)]
                for j in range(XG):
                    c = g * XG + j
                    for i, (h, w, k) in enumerate(passes):
                        last = pe.matmul(seg_ps[g % 2][:, j * D:(j + 1) * D], h[:, k, c * P:(c + 1) * P],
                                         w[:, k, :], start=(i == 0), stop=(i == len(passes) - 1))
                last.then_inc(v_ps_ready, 1)

            def weigh(b, g):
                if g == 0:
                    wait_reuse(pe, attn_ready, b)
                pe.wait_ge(lo_ready, GROUPS * b + g + 1)
                for c in range(g * GC, (g + 1) * GC):
                    for t in range(QT):
                        tile = slice(t * P, (t + 1) * P)
                        pe.matmul(acc_ps[t][:, 0:D + 1], p_hi[:, c, tile], v_hi[:, c, 0:D + 1],
                                  start=(c == 0), stop=False)
                        pe.matmul(acc_ps[t][:, 0:D], p_hi[:, c, tile], v_lo[:, c, :], start=False, stop=False)
                        last = pe.matmul(acc_ps[t][:, 0:D + 1], p_lo[:, c, tile], v_hi[:, c, 0:D + 1],
                                         start=False, stop=(c == CHUNKS - 1))
                last.then_inc(weighted, 1)

            def stage(i, par):
                if exists(i):
                    pe.wait_ge(g_ready, i + 1)
                for g in range(GROUPS):
                    if exists(i):
                        scores(i, g)
                    if g == 0 and exists(i - 1):
                        turn_max(i - 1)
                    if g == GROUPS - 1 and exists(i + 1):
                        project_g(i + 1)
                    if exists(i - 2):
                        weigh(i - 2, g)
                    if g == 0 and exists(i - 1):
                        spread_max(i - 1)
                if isinstance(i, int) and i == 0:
                    for g in range(XGROUPS):
                        project_v(g)
                    pe.wait_ge(v_ready, XGROUPS)

            pe.wait_ge(weights_split, 1)
            pe.wait_ge(hT_ready, XGROUPS)
            project_g(0)
            stages(pe, stage)


def kernel(x, adj, L0_gnn_Wq, L0_gnn_Wk, L0_gnn_Wv):
    import numpy as np
    import concourse.bacc as bacc
    from concourse.bass_utils import run_bass_kernel_spmd

    nc = bacc.Bacc("TRN2", target_bir_lowering=False, num_devices=1)
    arrays, args = {}, []
    for name, a in (("x", x), ("adj", adj), ("Wq", L0_gnn_Wq), ("Wk", L0_gnn_Wk), ("Wv", L0_gnn_Wv)):
        a = np.ascontiguousarray(a)
        arrays[f"in_{name}"] = a
        args.append(nc.dram_tensor(f"in_{name}", a.shape, mybir.dt.from_np(a.dtype), kind="ExternalInput").ap())
    out = nc.dram_tensor("out", arrays["in_x"].shape, F32, kind="ExternalOutput").ap()
    attention_layer(nc, *args, out)
    r = run_bass_kernel_spmd(nc, [arrays], core_ids=[0])
    return r.results[0]["out"]
```

```python
import math
from contextlib import ExitStack

import concourse.bass as bass
from concourse import mybir

ALU = mybir.AluOpType
ACT = mybir.ActivationFunctionType
AX_X = mybir.AxisListType.X
F32 = mybir.dt.float32
F16 = mybir.dt.float16
U8 = mybir.dt.uint8

P = 128
LN_EPS = 1e-5
MASKED = -1e30
NO_EDGE_MAX = -1e29
OPERAND_SCALE = 1024.0
SQUARES_FLOOR = 1e-36
LOG_P_SCALE = 14 * math.log(2.0)


def attention_layer(nc, x, adj, Wq, Wk, Wv, out):
    N, D = x.shape
    KC = D // P
    CHUNKS = N // P
    Q = 256
    QT = Q // P
    BLOCKS = N // Q
    BANK = 512
    SEG_CHUNKS = 4
    SEGS = CHUNKS // SEG_CHUNKS
    GROUPS = 4
    GC = CHUNKS // GROUPS
    XG = 4
    XGROUPS = CHUNKS // XG
    BATCHES = [(0, 1), (1, 2)] + [(g, g + 2) for g in range(2, XGROUPS, 2)]
    ACT_CHUNKS = 1
    assert KC == 2 and QT == 2 and GC == 2 * SEG_CHUNKS and XG * P == BANK and Q == D

    x_chunks = x.rearrange("(c p) d -> p c d", p=P)
    adj_chunks = adj.rearrange("(c p) i -> p c i", p=P)

    with ExitStack() as ctx:
        def sb(name, shape, dt):
            return ctx.enter_context(nc.sbuf_tensor(name, shape, dt))

        def ps(name, shape):
            return ctx.enter_context(nc.psum_tensor(name, shape, F32))

        def sem(name):
            return ctx.enter_context(nc.semaphore(name))

        hT_hi = sb("hT_hi", [P, KC, N], F16)
        hT_lo = sb("hT_lo", [P, KC, N], F16)
        v_hi = sb("v_hi", [P, CHUNKS, D + 2], F16)
        v_lo = sb("v_lo", [P, CHUNKS, D], F16)
        gT_hi = sb("gT_hi", [P, KC, Q], F16)
        gT_lo = sb("gT_lo", [P, KC, Q], F16)
        score = [sb(f"score{i}", [P, CHUNKS, Q], F32) for i in range(2)]
        x_in = score[1]
        p_hi = sb("p_hi", [P, CHUNKS, Q], F16)
        p_lo = sb("p_lo", [P, CHUNKS, Q], F16)
        edges = [sb(f"edges{i}", [P, CHUNKS, Q], U8) for i in range(2)]
        wq, wk, wv, squares = (p_hi[:, 4 * i:4 * (i + 1), :].rearrange("p c q -> p (c q)").bitcast(F32)
                               .rearrange("p (k d) -> p k d", k=KC) for i in range(4))
        v_f = [p_lo[:, 8 * i:8 * (i + 1), :].rearrange("p c q -> p (c q)").bitcast(F32)
               .rearrange("p (c d) -> p c d", d=D) for i in range(2)]
        a_hi = sb("a_hi", [P, KC, D], F16)
        a_lo = sb("a_lo", [P, KC, D], F16)
        wvT_hi = sb("wvT_hi", [P, KC, D], F16)
        wvT_lo = sb("wvT_lo", [P, KC, D], F16)
        ident = sb("ident", [P, P], F32)
        ones = sb("ones", [P, P], F32)
        norm_diag = sb("norm_diag", [P, KC, P], F32)
        v_scale_row = sb("v_scale_row", [P, D], F32)
        wv_sumsq = sb("wv_sumsq", [P, KC], F32)
        a_sumsq = sb("a_sumsq", [P, 1], F32)
        squares_floor = sb("squares_floor", [P, 1], F32)
        wv_norm = sb("wv_norm", [P, KC], F32)
        inv_wv_norm = sb("inv_wv_norm", [P, KC], F32)
        a_norm = sb("a_norm", [P, 1], F32)
        inv_a_norm = sb("inv_a_norm", [P, 1], F32)
        log_p_scale = sb("log_p_scale", [P, 1], F32)
        stats = sb("stats", [P, CHUNKS, 6], F32)
        mean_var = sb("mean_var", [P, CHUNKS, 2], F32)
        var_eps = sb("var_eps", [P, CHUNKS], F32)
        std = sb("std", [P, CHUNKS], F32)
        rstd0 = sb("rstd0", [P, CHUNKS], F32)
        newton = sb("newton", [P, CHUNKS], F32)
        rstd = sb("rstd", [P, CHUNKS], F32)
        shift_x = sb("shift_x", [P, CHUNKS], F32)
        group_max = sb("group_max", [P, GROUPS, Q], F32)
        block_max = sb("block_max", [P, Q], F32)
        query_max = sb("query_max", [P, QT], F32)
        max_diag = sb("max_diag", [P, QT, P], F32)
        max_row = sb("max_row", [P, Q], F32)
        sums = sb("sums", [P, QT], F32)
        inv_sums = sb("inv_sums", [P, QT], F32)
        attn = sb("attn", [P, QT, D], F32)
        x_res = sb("x_res", [P, QT, D], F32)
        y = sb("y", [P, QT, D], F32)

        seg_ps = [ps(f"seg_ps{i}", [P, 2 * BANK]) for i in range(2)]
        acc_ps = [ps(f"acc_ps{i}", [P, BANK]) for i in range(QT)]
        xT_ps = acc_ps
        g_ps = ps("g_ps", [P, KC * Q])
        max_ps = ps("max_ps", [P, BANK])
        a_ps, wvT_ps = g_ps, seg_ps[1]

        x_loaded = [sem(f"x_loaded{g}") for g in range(XGROUPS)]
        wqk_loaded = sem("wqk_loaded")
        wv_loaded = sem("wv_loaded")
        edges_loaded = sem("edges_loaded")
        x_res_loaded = sem("x_res_loaded")
        y_stored = sem("y_stored")
        zeroed = sem("zeroed")
        consts_ready = sem("consts_ready")
        a_ps_ready = sem("a_ps_ready")
        a_sumsq_ready = sem("a_sumsq_ready")
        a_total_ready = sem("a_total_ready")
        a_norm_ready = sem("a_norm_ready")
        inv_a_ready = sem("inv_a_ready")
        a_hi_ready = sem("a_hi_ready")
        a_ready = sem("a_ready")
        wv_sumsq_ready = sem("wv_sumsq_ready")
        wv_norm_ready = sem("wv_norm_ready")
        inv_wv_ready = sem("inv_wv_ready")
        wv_scaled = sem("wv_scaled")
        wvT_ready = sem("wvT_ready")
        wvT_hi_ready = sem("wvT_hi_ready")
        norm_row_ready = sem("norm_row_ready")
        wv_ready = sem("wv_ready")
        var_ready = sem("var_ready")
        std_ready = sem("std_ready")
        rstd_ready = sem("rstd_ready")
        xn_ready = sem("xn_ready")
        xn_rest_ready = sem("xn_rest_ready")
        xT_ready = sem("xT_ready")
        hT_hi_ready = sem("hT_hi_ready")
        hT_ready = sem("hT_ready")
        v_ps_ready = sem("v_ps_ready")
        v_read = sem("v_read")
        v_ready = sem("v_ready")
        g_ps_ready = sem("g_ps_ready")
        g_hi_ready = sem("g_hi_ready")
        g_ready = sem("g_ready")
        block_max_ready = sem("block_max_ready")
        max_turned = sem("max_turned")
        max_diag_ready = sem("max_diag_ready")
        max_row_ps_ready = sem("max_row_ps_ready")
        max_row_ready = sem("max_row_ready")
        attn_ready = sem("attn_ready")
        y_ready = sem("y_ready")
        scores_ready = sem("scores_ready")
        scores_masked = sem("scores_masked")
        filled = sem("filled")
        shifted = sem("shifted")
        shifted_first = sem("shifted_first")
        exp_ready = sem("exp_ready")
        hi_ready = sem("hi_ready")
        lo_ready = sem("lo_ready")
        weighted = sem("weighted")
        dve_step = sem("dve_step")

        def wait_reuse(engine, semaphore, value):
            if not isinstance(value, int) or value > 0:
                engine.wait_ge(semaphore, value)

        def wait_alone(engine, semaphore, value):
            wait_reuse(engine, semaphore, value)
            engine.nop(nofuse=True)

        LOOP_FROM, LOOP_TO = 4, BLOCKS - 2

        def stages(engine, stage):
            for i in range(1, LOOP_FROM):
                stage(i, i % 2)
            with engine.Fori(LOOP_FROM, LOOP_TO, 2) as i:
                stage(i, 0)
                stage(i + 1, 1)
            for i in range(LOOP_TO, BLOCKS + 2):
                stage(i, i % 2)

        def batch_of(g):
            return next(n for n, (first, end) in enumerate(BATCHES) if first <= g < end)

        def exists(block):
            return not isinstance(block, int) or 0 <= block < BLOCKS

        def is_last(b):
            return isinstance(b, int) and b == BLOCKS - 1

        def sums_ps(b, t):
            return seg_ps[0][:, t * BANK:(t + 1) * BANK] if is_last(b) else acc_ps[t]

        def segment_ps(b, s):
            return seg_ps[0 if isinstance(b, int) and b == 0 else s % 2]

        block = ctx.enter_context(nc.Block())

        @block.sync
        def _(sp):
            def load_x(g):
                sp.dma_start(x_in[:, g * XG:(g + 1) * XG, :],
                             x_chunks[:, g * XG:(g + 1) * XG, :]).then_inc(x_loaded[g], 16)

            load_x(0)
            for w_sb, w, loaded in ((wq, Wq, wqk_loaded), (wk, Wk, wqk_loaded), (wv, Wv, wv_loaded)):
                sp.dma_start(w_sb[:, :, :], w.rearrange("(c p) d -> p c d", p=P)).then_inc(loaded, 16)
            for g in range(1, XGROUPS):
                load_x(g)

            def load_edges(b, par):
                wait_alone(sp, edges_loaded, 16 * b)
                wait_alone(sp, scores_masked, SEGS * (b - 1))
                sp.dma_start(edges[par][:, :, :], adj_chunks[:, :, bass.ds(b * Q, Q)]).then_inc(edges_loaded, 16)

            def rows(t, b):
                return t[bass.ds(b * Q, Q), :].rearrange("(t p) d -> p t d", p=P)

            def load_residual(b):
                wait_alone(sp, y_ready, b)
                sp.dma_start(x_res[:, :, :], rows(x, b)).then_inc(x_res_loaded, 16)

            def store(b):
                wait_alone(sp, y_ready, b + 1)
                sp.dma_start(rows(out, b), y[:, :, :]).then_inc(y_stored, 16)

            def stage(i, par):
                if exists(i + 1):
                    load_edges(i + 1, 1 - par)
                if exists(i - 2):
                    load_residual(i - 2)
                    store(i - 2)

            load_edges(0, 0)
            stage(0, 0)
            stages(sp, stage)
            sp.wait_ge(y_stored, 16 * BLOCKS)

        @block.gpsimd
        def _(pool):
            pool.memset(ident[:, :], 0.0).then_inc(zeroed, 1)
            pool.memset(ones[:, :], 1.0)
            pool.memset(v_hi[:, :, D:D + 2], 1.0)
            pool.memset(log_p_scale[:, :], LOG_P_SCALE)
            pool.memset(squares_floor[:, :], SQUARES_FLOOR)
            pool.wait_ge(zeroed, 1)
            pool.affine_select(out=ident[:, :], in_=ident[:, :], compare_op=ALU.not_equal, fill=1.0,
                               base=0, pattern=[[-1, P]], channel_multiplier=1).then_inc(consts_ready, 1)

            def fill(par, g):
                pool.memset(score[par][:, g * GC:(g + 1) * GC, :], MASKED).then_inc(filled, 1)

            def shift(b, par, g):
                if g == (1 if is_last(b) else 0):
                    pool.wait_ge(max_row_ready, b + 1)
                group = score[par][:, g * GC:(g + 1) * GC, :]
                pool.tensor_tensor(group, group, max_row[:, None, :].to_broadcast([P, GC, Q]),
                                   ALU.subtract).then_inc(shifted, 1)

            def finish(b):
                pool.wait_ge(attn_ready, b + 1)
                pool.wait_ge(x_res_loaded, 16 * b + 16)
                wait_reuse(pool, y_stored, 16 * b)
                pool.tensor_tensor(y[:, :, :], attn[:, :, :], x_res[:, :, :], ALU.add).then_inc(y_ready, 1)

            def stage(i, par):
                for g in range(GROUPS):
                    if exists(i - 1) and not (is_last(i - 1) and g == 0):
                        shift(i - 1, 1 - par, g)
                    if g == 0 and exists(i) and not (isinstance(i, int) and i < 2):
                        wait_alone(pool, lo_ready, GROUPS * (i - 1))
                        fill(par, GROUPS - 1)
                for g in range(GROUPS - 1):
                    if exists(i + 1):
                        wait_alone(pool, lo_ready, GROUPS * (i - 1) + g + 1)
                        fill(1 - par, g)
                if exists(i - 2):
                    finish(i - 2)

            for g in range(GROUPS):
                fill(0, g)
            pool.wait_ge(inv_wv_ready, 1)
            for k in range(KC):
                pool.tensor_scalar(wv[:, k, :], wv[:, k, :], inv_wv_norm[:, k:k + 1], None, ALU.mult)
            for k in range(KC):
                last = pool.tensor_scalar(norm_diag[:, k, :], ident[:, :], wv_norm[:, k:k + 1], None, ALU.mult)
            last.then_inc(wv_scaled, 1)
            for g in range(XGROUPS):
                pool.wait_ge(v_read, g + 1)
                chunks = slice(g * XG, (g + 1) * XG)
                pool.tensor_tensor(v_lo[:, chunks, :], v_f[g % 2], v_hi[:, chunks, 0:D], ALU.subtract
                                   ).then_inc(v_ready, 1)
                if g == XGROUPS - 2:
                    pool.wait_ge(xT_ready, XGROUPS)
                if g >= XGROUPS - 2:
                    for h in range(2 * (g - XGROUPS + 2), 2 * (g - XGROUPS + 3)):
                        fill(1, h)
            stages(pool, stage)

        @block.scalar
        def _(act):
            def batch_std(n):
                act.wait_ge(var_ready, n + 1)
                cols = slice(BATCHES[n][0] * XG, BATCHES[n][1] * XG)
                act.activation(std[:, cols], var_eps[:, cols], ACT.Sqrt).then_inc(std_ready, 1)

            def normalise(g):
                act.wait_ge(rstd_ready, batch_of(g) + 1)
                for c in range(g * XG, (g + 1) * XG if g else ACT_CHUNKS):
                    last = act.activation(x_in[:, c, :], x_in[:, c, :], ACT.Identity,
                                          bias=shift_x[:, c:c + 1], scale=rstd[:, c:c + 1])
                last.then_inc(xn_ready, 1)

            def group_hT_hi(g):
                act.wait_ge(xT_ready, g + 1)
                for k in range(KC):
                    act.activation(hT_hi[:, k, g * BANK:(g + 1) * BANK], xT_ps[k][:, :],
                                   ACT.Relu).then_inc(hT_hi_ready, 1)

            act.preload_act_table(ACT.Sqrt)
            batch_std(0)
            normalise(0)
            act.wait_ge(a_ps_ready, 1)
            act.activation(squares[:, :, :].rearrange("p k d -> p (k d)"), a_ps[:, :], ACT.Square,
                           accum_out=a_sumsq[:, 0:1]).then_inc(a_sumsq_ready, 1)
            act.wait_ge(a_total_ready, 1)
            act.activation(a_norm[:, :], max_ps[:, 0:1], ACT.Sqrt, bias=squares_floor[:, 0:1],
                           scale=OPERAND_SCALE ** -2).then_inc(a_norm_ready, 1)
            act.wait_ge(inv_a_ready, 1)
            act.activation(a_hi[:, :, :].rearrange("p k d -> p (k d)"), a_ps[:, :], ACT.Copy,
                           scale=inv_a_norm[:, 0:1]).then_inc(a_hi_ready, 1)
            group_hT_hi(0)
            batch_std(1)
            act.wait_ge(wv_loaded, 16)
            act.wait_ge(a_sumsq_ready, 1)
            for k in range(KC):
                last = act.activation(squares[:, k, :], wv[:, k, :], ACT.Square, accum_out=wv_sumsq[:, k:k + 1])
            last.then_inc(wv_sumsq_ready, 1)
            act.wait_ge(wv_sumsq_ready, 1)
            act.activation(wv_norm[:, :], wv_sumsq[:, :], ACT.Sqrt, bias=squares_floor[:, 0:1],
                           scale=OPERAND_SCALE ** -2).then_inc(wv_norm_ready, 1)
            normalise(1)

            def split_g_hi(b):
                act.wait_ge(g_ps_ready, b + 1)
                wait_reuse(act, scores_ready, SEGS * b)
                act.activation(gT_hi[:, :, :].rearrange("p k d -> p (k d)"), g_ps[:, :], ACT.Copy
                               ).then_inc(g_hi_ready, 1)

            def take_max_row(b):
                act.wait_ge(max_row_ps_ready, b + 1)
                wait_reuse(act, shifted, GROUPS * b)
                act.activation(max_row[:, :], max_ps[:, Q:2 * Q], ACT.Copy).then_inc(max_row_ready, 1)

            def exponentials(b, par, g):
                if is_last(b):
                    act.wait_ge(*((shifted, GROUPS * b + g) if g else (shifted_first, 1)))
                else:
                    act.wait_ge(shifted, GROUPS * b + g + 1)
                group = score[par][:, g * GC:(g + 1) * GC, :].rearrange("p c q -> p (c q)")
                act.activation(group, group, ACT.Exp, bias=log_p_scale[:, 0:1],
                               scale=a_norm[:, 0:1]).then_inc(exp_ready, 1)

            def split_p_hi(b, par, g):
                act.wait_ge(exp_ready, GROUPS * b + g + 1)
                wait_reuse(act, weighted, GROUPS * (b - 1) + g + 1)
                act.activation(p_hi[:, g * GC:(g + 1) * GC, :].rearrange("p c q -> p (c q)"),
                               score[par][:, g * GC:(g + 1) * GC, :].rearrange("p c q -> p (c q)"),
                               ACT.Copy).then_inc(hi_ready, 1)

            def v_hi_of(g):
                act.wait_ge(v_ps_ready, g + 1)
                wait_reuse(act, v_ready, g - 1)
                v_ps = seg_ps[1][:, :].rearrange("p (c d) -> p c d", d=D)
                act.activation(v_hi[:, g * XG:(g + 1) * XG, 0:D], v_ps, ACT.Copy)
                act.activation(v_f[g % 2], v_ps, ACT.Copy).then_inc(v_read, 1)

            def stage(i, par):
                if exists(i - 1):
                    take_max_row(i - 1)
                for g in range(GROUPS):
                    if exists(i - 1):
                        exponentials(i - 1, 1 - par, g)
                    if g == GROUPS - 1 and exists(i + 1):
                        split_g_hi(i + 1)
                    if exists(i - 1):
                        split_p_hi(i - 1, 1 - par, g)

            split_g_hi(0)
            group_hT_hi(1)
            act.wait_ge(wvT_ready, 1)
            act.activation(wvT_hi[:, :, :].rearrange("p k d -> p (k d)"), wvT_ps[:, 0:KC * D],
                           ACT.Copy).then_inc(wvT_hi_ready, 1)
            for g in range(XGROUPS):
                if 0 < g < XGROUPS - 1:
                    group_hT_hi(g + 1)
                if g + 2 < XGROUPS:
                    if g in (0, 2, 4):
                        batch_std(2 + g // 2)
                    normalise(g + 2)
                if g == XGROUPS - 1:
                    split_g_hi(1)
                v_hi_of(g)
            stages(act, stage)

        @block.vector
        def _(dve):
            steps = [0]

            def step(instruction):
                instruction.then_inc(dve_step, 1)
                steps[0] = steps[0] + 1
                dve.wait_ge(dve_step, steps[0])

            def group_stats(g):
                dve.wait_ge(x_loaded[g], 16)
                for c in range(g * XG, (g + 1) * XG):
                    last = dve.bn_stats(stats[:, c, :], x_in[:, c, :])
                step(last)
                for c in range(g * XG, (g + 1) * XG):
                    last = dve.bn_aggr(mean_var[:, c, :], stats[:, c, :])
                step(last)

            def batch_var(n):
                cols = slice(BATCHES[n][0] * XG, BATCHES[n][1] * XG)
                dve.tensor_scalar(var_eps[:, cols], mean_var[:, cols, 1], LN_EPS, None,
                                  ALU.add).then_inc(var_ready, 1)

            def batch_rstd(n):
                cols = slice(BATCHES[n][0] * XG, BATCHES[n][1] * XG)
                dve.wait_ge(std_ready, n + 1)
                step(dve.reciprocal(rstd0[:, cols], std[:, cols]))
                step(dve.tensor_tensor(newton[:, cols], rstd0[:, cols], rstd0[:, cols], ALU.mult))
                step(dve.tensor_tensor(newton[:, cols], newton[:, cols], var_eps[:, cols], ALU.mult))
                step(dve.tensor_scalar(newton[:, cols], newton[:, cols], -0.5, 1.5, ALU.mult, ALU.add))
                step(dve.tensor_tensor(rstd[:, cols], newton[:, cols], rstd0[:, cols], ALU.mult))
                dve.scalar_tensor_tensor(shift_x[:, cols], mean_var[:, cols, 0], -1.0, rstd[:, cols],
                                         ALU.mult, ALU.mult).then_inc(rstd_ready, 1)

            def group_hT_lo(g):
                for k in range(KC):
                    dve.wait_ge(hT_hi_ready, KC * g + k + 1)
                    cols = slice(g * BANK, (g + 1) * BANK)
                    last = dve.scalar_tensor_tensor(hT_lo[:, k, cols], xT_ps[k][:, :], 0.0, hT_hi[:, k, cols],
                                                    ALU.max, ALU.subtract)
                last.then_inc(hT_ready, 1)

            def split_g_lo(b):
                dve.wait_ge(g_hi_ready, b + 1)
                dve.tensor_tensor(gT_lo[:, :, :].rearrange("p k d -> p (k d)"), g_ps[:, :],
                                  gT_hi[:, :, :].rearrange("p k d -> p (k d)"), ALU.subtract).then_inc(g_ready, 1)

            def mask(b, par, s):
                if s == 0:
                    dve.wait_ge(edges_loaded, 16 * b + 16)
                if s % 2 == 0:
                    dve.wait_ge(filled, GROUPS * b + s // 2 + 1)
                wait_alone(dve, scores_ready, SEGS * b + s + 1)
                chunks = slice(s * SEG_CHUNKS, (s + 1) * SEG_CHUNKS)
                dve.copy_predicated(score[par][:, chunks, :].rearrange("p c q -> p (c q)"),
                                    edges[par][:, chunks, :].rearrange("p c q -> p (c q)"),
                                    segment_ps(b, s)[:, :]).then_inc(scores_masked, 1)

            def max_over_group(b, par, g):
                dve.wait_ge(scores_masked, SEGS * b + 2 * g + 2)
                step(dve.reduce_max(group_max[:, g, :],
                                    score[par][:, g * GC:(g + 1) * GC, :].rearrange("p c q -> p q c"), AX_X))

            def max_over_chunks():
                dve.reduce_max(block_max[:, :], group_max[:, :, :].rearrange("p g q -> p q g"),
                               AX_X).then_inc(block_max_ready, 1)

            def max_over_partitions(b):
                dve.wait_ge(max_turned, b + 1)
                step(dve.reduce_max(query_max[:, :], max_ps[:, 0:Q].rearrange("p (t k) -> p t k", t=QT), AX_X))
                step(dve.tensor_scalar(query_max[:, :], query_max[:, :], NO_EDGE_MAX, None, ALU.max))
                for t in range(QT):
                    last = dve.tensor_scalar(max_diag[:, t, :], ident[:, :], query_max[:, t:t + 1], None, ALU.mult)
                last.then_inc(max_diag_ready, 1)

            def shift_first(b, par):
                dve.wait_ge(max_row_ready, b + 1)
                group = score[par][:, 0:GC, :]
                dve.tensor_tensor(group, group, max_row[:, None, :].to_broadcast([P, GC, Q]),
                                  ALU.subtract).then_inc(shifted_first, 1)

            def split_p_lo(b, par, g):
                dve.wait_ge(hi_ready, GROUPS * b + g + 1)
                chunks = slice(g * GC, (g + 1) * GC)
                dve.tensor_tensor(p_lo[:, chunks, :], score[par][:, chunks, :], p_hi[:, chunks, :],
                                  ALU.subtract).then_inc(lo_ready, 1)

            def scale_sums(b):
                dve.wait_ge(weighted, GROUPS * (b + 1))
                for t in range(QT):
                    last = dve.tensor_scalar(sums[:, t:t + 1], sums_ps(b, t)[:, D:D + 1], 1.0, None, ALU.max)
                step(last)
                step(dve.reciprocal(inv_sums[:, :], sums[:, :]))
                wait_reuse(dve, y_ready, b)
                for t in range(QT):
                    last = dve.scalar_tensor_tensor(attn[:, t, :], sums_ps(b, t)[:, 0:D], inv_sums[:, t:t + 1],
                                                    v_scale_row[:, :], ALU.mult, ALU.mult)
                last.then_inc(attn_ready, 1)

            STAGE_STEPS = GROUPS + 2 + 2

            def stage(i, par):
                if not isinstance(i, int) and par == 0:
                    steps[0] = loop_base[0] + (i - LOOP_FROM) * STAGE_STEPS
                for g in range(GROUPS):
                    if g == GROUPS // 2 and exists(i - 2):
                        scale_sums(i - 2)
                    if exists(i):
                        mask(i, par, 2 * g)
                    if g == 0 and exists(i - 1):
                        max_over_partitions(i - 1)
                    if exists(i):
                        mask(i, par, 2 * g + 1)
                        max_over_group(i, par, g)
                    if g == GROUPS - 1:
                        if exists(i + 1):
                            split_g_lo(i + 1)
                        if exists(i):
                            max_over_chunks()
                    if g == 0 and is_last(i - 1):
                        shift_first(i - 1, 1 - par)
                    if g == 0 and exists(i - 2):
                        split_p_lo(i - 2, par, GROUPS - 1)
                    if g > 0 and exists(i - 1):
                        split_p_lo(i - 1, 1 - par, g - 1)
                if isinstance(i, int) and i == LOOP_FROM - 1:
                    loop_base[0] = steps[0]

            loop_base = [0]
            group_stats(0)
            batch_var(0)
            batch_rstd(0)
            dve.wait_ge(rstd_ready, 1)
            for c in range(ACT_CHUNKS, XG):
                last = dve.tensor_scalar(x_in[:, c, :], x_in[:, c, :], rstd[:, c:c + 1], shift_x[:, c:c + 1],
                                         ALU.mult, ALU.add)
            last.then_inc(xn_rest_ready, 1)
            group_stats(1)
            batch_var(1)
            dve.wait_ge(a_norm_ready, 1)
            dve.reciprocal(inv_a_norm[:, :], a_norm[:, :]).then_inc(inv_a_ready, 1)
            dve.wait_ge(inv_a_ready, 1)
            dve.wait_ge(a_hi_ready, 1)
            dve.scalar_tensor_tensor(a_lo[:, :, :].rearrange("p k d -> p (k d)"), a_ps[:, :], inv_a_norm[:, 0:1],
                                     a_hi[:, :, :].rearrange("p k d -> p (k d)"),
                                     ALU.mult, ALU.subtract).then_inc(a_ready, 1)
            group_hT_lo(0)
            batch_rstd(1)
            dve.wait_ge(wv_norm_ready, 1)
            dve.reciprocal(inv_wv_norm[:, :], wv_norm[:, :]).then_inc(inv_wv_ready, 1)
            group_stats(2)
            split_g_lo(0)
            group_hT_lo(1)
            group_stats(3)
            batch_var(2)
            dve.wait_ge(wvT_hi_ready, 1)
            dve.tensor_tensor(wvT_lo[:, :, :].rearrange("p k d -> p (k d)"), wvT_ps[:, 0:KC * D],
                              wvT_hi[:, :, :].rearrange("p k d -> p (k d)"), ALU.subtract).then_inc(wv_ready, 1)
            for g in range(XGROUPS):
                if 0 < g < XGROUPS - 1:
                    group_hT_lo(g + 1)
                if g in (0, 2, 4):
                    batch_rstd(2 + g // 2)
                mask(0, 0, g)
                if g == 0:
                    dve.wait_ge(norm_row_ready, 1)
                    dve.tensor_copy(v_scale_row[:, :], max_ps[:, Q:Q + D])
                if g == XGROUPS - 1:
                    split_g_lo(1)
                if g % 2:
                    max_over_group(0, 0, g // 2)
                if g + 4 < XGROUPS:
                    group_stats(g + 4)
                    if g % 2:
                        batch_var(3 + g // 2)
            max_over_chunks()
            for i in range(1, LOOP_FROM):
                stage(i, i % 2)
            with dve.Fori(LOOP_FROM, LOOP_TO, 2) as i:
                stage(i, 0)
                stage(i + 1, 1)
            steps[0] = loop_base[0] + (LOOP_TO - LOOP_FROM) * STAGE_STEPS
            for i in range(LOOP_TO, BLOCKS + 2):
                stage(i, i % 2)

        @block.tensor
        def _(pe):
            def turn_x(g):
                pe.wait_ge(xn_ready, g + 1)
                if g == 0:
                    pe.wait_ge(xn_rest_ready, 1)
                wait_reuse(pe, hT_ready, g)
                for k in range(KC):
                    for c in range(XG):
                        last = pe.transpose(xT_ps[k][:, c * P:(c + 1) * P],
                                            x_in[:, g * XG + c, k * P:(k + 1) * P], ident[:, :])
                last.then_inc(xT_ready, 1)

            pe.wait_ge(consts_ready, 1)
            pe.wait_ge(wqk_loaded, 32)
            for m in range(KC):
                for k in range(KC):
                    last = pe.matmul(a_ps[:, m * D:(m + 1) * D], wq[:, k, m * P:(m + 1) * P], wk[:, k, :],
                                     start=(k == 0), stop=(k == KC - 1))
            last.then_inc(a_ps_ready, 1)
            turn_x(0)
            pe.wait_ge(a_sumsq_ready, 1)
            pe.matmul(max_ps[:, 0:1], ones[:, :], a_sumsq[:, 0:1], start=True, stop=True).then_inc(a_total_ready, 1)

            def turn_wv():
                pe.wait_ge(wv_scaled, 1)
                for k in range(KC):
                    for m in range(KC):
                        last = pe.transpose(wvT_ps[:, m * D + k * P:m * D + (k + 1) * P],
                                            wv[:, k, m * P:(m + 1) * P], ident[:, :])
                last.then_inc(wvT_ready, 1)
                for k in range(KC):
                    last = pe.matmul(max_ps[:, Q + k * P:Q + (k + 1) * P], ones[:, :], norm_diag[:, k, :],
                                     start=True, stop=True)
                last.then_inc(norm_row_ready, 1)

            def project_g(b):
                passes = [(a, h, k) for a, h in ((a_hi, hT_hi), (a_hi, hT_lo), (a_lo, hT_hi)) for k in range(KC)]
                for m in range(KC):
                    for i, (a, h, k) in enumerate(passes):
                        last = pe.matmul(g_ps[:, m * Q:(m + 1) * Q], a[:, k, m * P:(m + 1) * P],
                                         h[:, k, bass.ds(b * Q, Q)],
                                         start=(i == 0), stop=(i == len(passes) - 1))
                last.then_inc(g_ps_ready, 1)

            def scores(b, s):
                passes = [(h, q, k) for h, q in ((hT_hi, gT_hi), (hT_hi, gT_lo), (hT_lo, gT_hi)) for k in range(KC)]
                for j in range(SEG_CHUNKS):
                    c = s * SEG_CHUNKS + j
                    for i, (h, q, k) in enumerate(passes):
                        last = pe.matmul(segment_ps(b, s)[:, j * Q:(j + 1) * Q], h[:, k, c * P:(c + 1) * P],
                                         q[:, k, :], start=(i == 0), stop=(i == len(passes) - 1))
                last.then_inc(scores_ready, 1)

            def turn_max(b):
                pe.wait_ge(block_max_ready, b + 1)
                wait_reuse(pe, max_row_ready, b)
                for t in range(QT):
                    last = pe.transpose(max_ps[:, t * P:(t + 1) * P], block_max[:, t * P:(t + 1) * P], ident[:, :])
                last.then_inc(max_turned, 1)

            def spread_max(b):
                pe.wait_ge(max_diag_ready, b + 1)
                for t in range(QT):
                    last = pe.matmul(max_ps[:, Q + t * P:Q + (t + 1) * P], ones[:, :], max_diag[:, t, :],
                                     start=True, stop=True)
                last.then_inc(max_row_ps_ready, 1)

            def project_v(g):
                wait_reuse(pe, v_read, g)
                passes = [(h, w, k) for h, w in ((hT_hi, wvT_hi), (hT_hi, wvT_lo), (hT_lo, wvT_hi)) for k in range(KC)]
                for j in range(XG):
                    c = g * XG + j
                    for i, (h, w, k) in enumerate(passes):
                        last = pe.matmul(seg_ps[1][:, j * D:(j + 1) * D], h[:, k, c * P:(c + 1) * P],
                                         w[:, k, :], start=(i == 0), stop=(i == len(passes) - 1))
                last.then_inc(v_ps_ready, 1)

            def weigh(b, g, turning=None):
                if g == 0 and not is_last(b):
                    wait_reuse(pe, attn_ready, b)
                if isinstance(b, int) and b == 0:
                    pe.wait_ge(v_ready, 2 * (g + 1))
                pe.wait_ge(lo_ready, GROUPS * b + g + 1)
                for c in range(g * GC, (g + 1) * GC):
                    if turning is not None and c == g * GC + GC // 2:
                        spread_max(turning)
                    for t in range(QT):
                        tile = slice(t * P, (t + 1) * P)
                        pe.matmul(sums_ps(b, t)[:, 0:D + 1], p_hi[:, c, tile], v_hi[:, c, 0:D + 1],
                                  start=(c == 0), stop=False)
                        pe.matmul(sums_ps(b, t)[:, 0:D], p_hi[:, c, tile], v_lo[:, c, :], start=False, stop=False)
                        last = pe.matmul(sums_ps(b, t)[:, 0:D + 1], p_lo[:, c, tile], v_hi[:, c, 0:D + 1],
                                         start=False, stop=(c == CHUNKS - 1))
                last.then_inc(weighted, 1)

            def stage(i, par):
                if exists(i):
                    pe.wait_ge(g_ready, i + 1)
                for g in range(GROUPS):
                    if exists(i):
                        for s in (2 * g, 2 * g + 1):
                            if isinstance(i, int) and i == 1 and s < 2:
                                pe.wait_ge(*((scores_masked, SEGS), (v_read, XGROUPS))[s])
                            else:
                                pe.wait_ge(scores_masked, SEGS * i + s - 1)
                            scores(i, s)
                    if g == 0 and exists(i - 1):
                        turn_max(i - 1)
                    if g == GROUPS - 1 and exists(i + 1):
                        project_g(i + 1)
                    b = i - 2 if g < GROUPS // 2 else i - 1
                    turning = i - 1 if g == 0 and exists(i - 1) else None
                    if exists(b):
                        weigh(b, (g + GROUPS // 2) % GROUPS, turning)
                    elif turning is not None:
                        spread_max(turning)

            pe.wait_ge(a_ready, 1)
            pe.wait_ge(hT_ready, 1)
            project_g(0)
            turn_x(1)
            turn_wv()
            pe.wait_ge(g_ready, 1)
            for g in range(XGROUPS):
                if g > 0 and g + 1 < XGROUPS:
                    turn_x(g + 1)
                pe.wait_ge(hT_ready, g + 1)
                wait_reuse(pe, scores_masked, g)
                scores(0, g)
                if g == 0:
                    pe.wait_ge(wv_ready, 1)
                if g == XGROUPS - 1:
                    project_g(1)
                project_v(g)
            stages(pe, stage)


def kernel(x, adj, L0_gnn_Wq, L0_gnn_Wk, L0_gnn_Wv):
    import numpy as np
    import concourse.bacc as bacc
    from concourse.bass_utils import run_bass_kernel_spmd

    nc = bacc.Bacc("TRN2", target_bir_lowering=False, num_devices=1)
    arrays, args = {}, []
    for name, a in (("x", x), ("adj", adj), ("Wq", L0_gnn_Wq), ("Wk", L0_gnn_Wk), ("Wv", L0_gnn_Wv)):
        a = np.ascontiguousarray(a)
        arrays[f"in_{name}"] = a
        args.append(nc.dram_tensor(f"in_{name}", a.shape, mybir.dt.from_np(a.dtype), kind="ExternalInput").ap())
    out = nc.dram_tensor("out", arrays["in_x"].shape, F32, kind="ExternalOutput").ap()
    attention_layer(nc, *args, out)
    r = run_bass_kernel_spmd(nc, [arrays], core_ids=[0])
    return r.results[0]["out"]
```

```python
import math
from contextlib import ExitStack

import concourse.bass as bass
from concourse import mybir

ALU = mybir.AluOpType
ACT = mybir.ActivationFunctionType
AX_X = mybir.AxisListType.X
F32 = mybir.dt.float32
F16 = mybir.dt.float16
U8 = mybir.dt.uint8

P = 128
LN_EPS = 1e-5
MASKED = -1e30
NO_EDGE_MAX = -1e29
OPERAND_SCALE = 1024.0
SQUARES_FLOOR = 1e-36
LOG_P_SCALE = 14 * math.log(2.0)


def attention_layer(nc, x, adj, Wq, Wk, Wv, out):
    N, D = x.shape
    KC = D // P
    CHUNKS = N // P
    Q = 256
    QT = Q // P
    BLOCKS = N // Q
    BANK = 512
    SEG_CHUNKS = 4
    SEGS = CHUNKS // SEG_CHUNKS
    GROUPS = 4
    GC = CHUNKS // GROUPS
    XG = 4
    XGROUPS = CHUNKS // XG
    BATCHES = [(0, 1), (1, 2)] + [(g, g + 2) for g in range(2, XGROUPS, 2)]
    WARM_UP = 10
    ACT_CHUNKS = 1
    assert KC == 2 and QT == 2 and GC == 2 * SEG_CHUNKS and XG * P == BANK and Q == D

    x_chunks = x.rearrange("(c p) d -> p c d", p=P)
    adj_chunks = adj.rearrange("(c p) i -> p c i", p=P)

    with ExitStack() as ctx:
        def sb(name, shape, dt):
            return ctx.enter_context(nc.sbuf_tensor(name, shape, dt))

        def ps(name, shape):
            return ctx.enter_context(nc.psum_tensor(name, shape, F32))

        def sem(name):
            return ctx.enter_context(nc.semaphore(name))

        hT_hi = sb("hT_hi", [P, KC, N], F16)
        hT_lo = sb("hT_lo", [P, KC, N], F16)
        v_hi = sb("v_hi", [P, CHUNKS, D + 2], F16)
        v_lo = sb("v_lo", [P, CHUNKS, D], F16)
        gT_hi = sb("gT_hi", [P, KC, Q], F16)
        gT_lo = sb("gT_lo", [P, KC, Q], F16)
        score = [sb(f"score{i}", [P, CHUNKS, Q], F32) for i in range(2)]
        x_in = score[1]
        p_hi = sb("p_hi", [P, CHUNKS, Q], F16)
        p_lo = sb("p_lo", [P, CHUNKS, Q], F16)
        edges = [sb(f"edges{i}", [P, CHUNKS, Q], U8) for i in range(2)]
        wq, wk, wv, squares = (p_hi[:, 4 * i:4 * (i + 1), :].rearrange("p c q -> p (c q)").bitcast(F32)
                               .rearrange("p (k d) -> p k d", k=KC) for i in range(4))
        v_f = [p_lo[:, 8 * i:8 * (i + 1), :].rearrange("p c q -> p (c q)").bitcast(F32)
               .rearrange("p (c d) -> p c d", d=D) for i in range(2)]
        a_hi = sb("a_hi", [P, KC, D], F16)
        a_lo = sb("a_lo", [P, KC, D], F16)
        wvT_hi = sb("wvT_hi", [P, KC, D], F16)
        wvT_lo = sb("wvT_lo", [P, KC, D], F16)
        ident = sb("ident", [P, P], F32)
        ones = sb("ones", [P, P], F32)
        norm_diag = sb("norm_diag", [P, KC, P], F32)
        v_scale_row = sb("v_scale_row", [P, D], F32)
        wv_sumsq = sb("wv_sumsq", [P, KC], F32)
        a_sumsq = sb("a_sumsq", [P, 1], F32)
        squares_floor = sb("squares_floor", [P, 1], F32)
        wv_norm = sb("wv_norm", [P, KC], F32)
        inv_wv_norm = sb("inv_wv_norm", [P, KC], F32)
        a_norm = sb("a_norm", [P, 1], F32)
        inv_a_norm = sb("inv_a_norm", [P, 1], F32)
        log_p_scale = sb("log_p_scale", [P, 1], F32)
        stats = sb("stats", [P, CHUNKS, 6], F32)
        mean_var = sb("mean_var", [P, CHUNKS, 2], F32)
        var_eps = sb("var_eps", [P, CHUNKS], F32)
        std = sb("std", [P, CHUNKS], F32)
        rstd0 = sb("rstd0", [P, CHUNKS], F32)
        newton = sb("newton", [P, CHUNKS], F32)
        rstd = sb("rstd", [P, CHUNKS], F32)
        shift_x = sb("shift_x", [P, CHUNKS], F32)
        group_max = sb("group_max", [P, GROUPS, Q], F32)
        block_max = sb("block_max", [P, Q], F32)
        query_max = sb("query_max", [P, QT], F32)
        max_diag = sb("max_diag", [P, QT, P], F32)
        max_row = sb("max_row", [P, Q], F32)
        sums = sb("sums", [P, QT], F32)
        inv_sums = sb("inv_sums", [P, QT], F32)
        attn = sb("attn", [P, QT, D], F32)
        x_res = sb("x_res", [P, QT, D], F32)
        y = sb("y", [P, QT, D], F32)

        seg_ps = [ps(f"seg_ps{i}", [P, 2 * BANK]) for i in range(2)]
        acc_ps = [ps(f"acc_ps{i}", [P, BANK]) for i in range(QT)]
        xT_ps = acc_ps
        g_ps = ps("g_ps", [P, KC * Q])
        max_ps = ps("max_ps", [P, BANK])
        a_ps, wvT_ps = g_ps, seg_ps[1]

        x_loaded = [sem(f"x_loaded{g}") for g in range(XGROUPS)]
        wqk_loaded = sem("wqk_loaded")
        wv_loaded = sem("wv_loaded")
        edges_loaded = sem("edges_loaded")
        x_res_loaded = sem("x_res_loaded")
        y_stored = sem("y_stored")
        zeroed = sem("zeroed")
        consts_ready = sem("consts_ready")
        a_ps_ready = sem("a_ps_ready")
        a_sumsq_ready = sem("a_sumsq_ready")
        a_total_ready = sem("a_total_ready")
        a_norm_ready = sem("a_norm_ready")
        inv_a_ready = sem("inv_a_ready")
        a_hi_ready = sem("a_hi_ready")
        a_ready = sem("a_ready")
        wv_sumsq_ready = sem("wv_sumsq_ready")
        wv_norm_ready = sem("wv_norm_ready")
        wv_scaled = sem("wv_scaled")
        norm_diag_ready = sem("norm_diag_ready")
        wvT_ready = sem("wvT_ready")
        wvT_hi_ready = sem("wvT_hi_ready")
        norm_row_ready = sem("norm_row_ready")
        wv_ready = sem("wv_ready")
        var_ready = sem("var_ready")
        std_ready = sem("std_ready")
        rstd_ready = sem("rstd_ready")
        xn_ready = sem("xn_ready")
        xn_rest_ready = sem("xn_rest_ready")
        xT_ready = sem("xT_ready")
        hT_hi_ready = sem("hT_hi_ready")
        hT_ready = sem("hT_ready")
        v_ps_ready = sem("v_ps_ready")
        v_read = sem("v_read")
        v_ready = sem("v_ready")
        g_ps_ready = sem("g_ps_ready")
        g_hi_ready = sem("g_hi_ready")
        g_ready = sem("g_ready")
        block_max_ready = sem("block_max_ready")
        max_turned = sem("max_turned")
        max_diag_ready = sem("max_diag_ready")
        max_row_ps_ready = sem("max_row_ps_ready")
        max_row_ready = sem("max_row_ready")
        attn_ready = sem("attn_ready")
        y_ready = sem("y_ready")
        scores_ready = sem("scores_ready")
        scores_masked = sem("scores_masked")
        filled = sem("filled")
        shifted = sem("shifted")
        exp_ready = sem("exp_ready")
        hi_ready = sem("hi_ready")
        lo_ready = sem("lo_ready")
        weighted = sem("weighted")
        tile_weighted = sem("tile_weighted")
        tile_y_ready = sem("tile_y_ready")
        dve_step = sem("dve_step")

        def wait_reuse(engine, semaphore, value):
            if not isinstance(value, int) or value > 0:
                engine.wait_ge(semaphore, value)

        def wait_alone(engine, semaphore, value):
            wait_reuse(engine, semaphore, value)
            engine.nop(nofuse=True)

        LOOP_FROM, LOOP_TO = 4, BLOCKS - 2

        def stages(engine, stage):
            for i in range(1, LOOP_FROM):
                stage(i, i % 2)
            with engine.Fori(LOOP_FROM, LOOP_TO, 2) as i:
                stage(i, 0)
                stage(i + 1, 1)
            for i in range(LOOP_TO, BLOCKS + 2):
                stage(i, i % 2)

        def batch_of(g):
            return next(n for n, (first, end) in enumerate(BATCHES) if first <= g < end)

        def exists(block):
            return not isinstance(block, int) or 0 <= block < BLOCKS

        def is_last(b):
            return isinstance(b, int) and b == BLOCKS - 1

        def sums_ps(b, t):
            return seg_ps[0][:, t * BANK:(t + 1) * BANK] if is_last(b) else acc_ps[t]

        def segment_ps(b, s):
            return seg_ps[0 if isinstance(b, int) and b == 0 else s % 2]

        block = ctx.enter_context(nc.Block())

        @block.sync
        def _(sp):
            def load_x(g):
                sp.dma_start(x_in[:, g * XG:(g + 1) * XG, :],
                             x_chunks[:, g * XG:(g + 1) * XG, :]).then_inc(x_loaded[g], 16)

            load_x(0)
            for w_sb, w, loaded in ((wq, Wq, wqk_loaded), (wk, Wk, wqk_loaded), (wv, Wv, wv_loaded)):
                sp.dma_start(w_sb[:, :, :], w.rearrange("(c p) d -> p c d", p=P)).then_inc(loaded, 16)
            for g in range(1, XGROUPS):
                load_x(g)

            def load_edges(b, par):
                wait_alone(sp, edges_loaded, 16 * b)
                wait_alone(sp, scores_masked, SEGS * (b - 1))
                sp.dma_start(edges[par][:, :, :], adj_chunks[:, :, bass.ds(b * Q, Q)]).then_inc(edges_loaded, 16)

            def rows(t, b):
                return t[bass.ds(b * Q, Q), :].rearrange("(t p) d -> p t d", p=P)

            def load_residual(b):
                wait_alone(sp, y_ready, b)
                sp.dma_start(x_res[:, :, :], rows(x, b)).then_inc(x_res_loaded, 16)

            def store(b):
                wait_alone(sp, y_ready, b + 1)
                sp.dma_start(rows(out, b), y[:, :, :]).then_inc(y_stored, 16)

            def stage(i, par):
                if exists(i + 1):
                    load_edges(i + 1, 1 - par)
                if exists(i - 2):
                    load_residual(i - 2)
                    if not is_last(i - 2):
                        store(i - 2)

            load_edges(0, 0)
            stage(0, 0)
            stages(sp, stage)
            for t in range(QT):
                sp.wait_ge(tile_y_ready, t + 1)
                sp.dma_start(out[(BLOCKS - 1) * Q + t * P:(BLOCKS - 1) * Q + (t + 1) * P, :],
                             y[:, t, :]).then_inc(y_stored, 16)
            sp.wait_ge(y_stored, 16 * (BLOCKS - 1 + QT))

        @block.gpsimd
        def _(pool):
            pool.memset(ident[:, :], 0.0).then_inc(zeroed, 1)
            pool.memset(ones[:, :], 1.0)
            pool.memset(v_hi[:, :, D:D + 2], 1.0)
            pool.memset(log_p_scale[:, :], LOG_P_SCALE)
            pool.memset(squares_floor[:, :], SQUARES_FLOOR)
            pool.wait_ge(zeroed, 1)
            pool.affine_select(out=ident[:, :], in_=ident[:, :], compare_op=ALU.not_equal, fill=1.0,
                               base=0, pattern=[[-1, P]], channel_multiplier=1).then_inc(consts_ready, 1)

            def fill(par, g):
                pool.memset(score[par][:, g * GC:(g + 1) * GC, :], MASKED).then_inc(filled, 1)

            def shift(b, par, g):
                if g == 0:
                    pool.wait_ge(max_row_ready, b + 1)
                group = score[par][:, g * GC:(g + 1) * GC, :]
                pool.tensor_tensor(group, group, max_row[:, None, :].to_broadcast([P, GC, Q]),
                                   ALU.subtract).then_inc(shifted, 1)

            def finish(b):
                pool.wait_ge(attn_ready, b + 1)
                pool.wait_ge(x_res_loaded, 16 * b + 16)
                wait_reuse(pool, y_stored, 16 * b)
                pool.tensor_tensor(y[:, :, :], attn[:, :, :], x_res[:, :, :], ALU.add).then_inc(y_ready, 1)

            def stage(i, par):
                for g in range(GROUPS):
                    if exists(i - 1):
                        shift(i - 1, 1 - par, g)
                    if g == 0 and exists(i) and not (isinstance(i, int) and i < 2):
                        wait_alone(pool, lo_ready, GROUPS * (i - 1))
                        fill(par, GROUPS - 1)
                for g in range(GROUPS - 1):
                    if exists(i + 1):
                        wait_alone(pool, lo_ready, GROUPS * (i - 1) + g + 1)
                        fill(1 - par, g)
                if exists(i - 2) and not is_last(i - 2):
                    finish(i - 2)

            for g in range(GROUPS):
                fill(0, g)
            pool.wait_ge(wv_norm_ready, 1)
            for k in range(KC):
                last = pool.tensor_scalar(norm_diag[:, k, :], ident[:, :], wv_norm[:, k:k + 1], None, ALU.mult)
            last.then_inc(norm_diag_ready, 1)
            for g in range(XGROUPS):
                pool.wait_ge(v_read, g + 1)
                chunks = slice(g * XG, (g + 1) * XG)
                pool.tensor_tensor(v_lo[:, chunks, :], v_f[g % 2], v_hi[:, chunks, 0:D], ALU.subtract
                                   ).then_inc(v_ready, 1)
                if g == XGROUPS - 2:
                    pool.wait_ge(xT_ready, XGROUPS)
                if g >= XGROUPS - 2:
                    for h in range(2 * (g - XGROUPS + 2), 2 * (g - XGROUPS + 3)):
                        fill(1, h)
            stages(pool, stage)

        @block.scalar
        def _(act):
            def batch_std(n):
                act.wait_ge(var_ready, n + 1)
                cols = slice(BATCHES[n][0] * XG, BATCHES[n][1] * XG)
                act.activation(std[:, cols], var_eps[:, cols], ACT.Sqrt).then_inc(std_ready, 1)

            def normalise(g, first=0, end=XG):
                act.wait_ge(rstd_ready, batch_of(g) + 1)
                for c in range(g * XG + first, g * XG + end):
                    act.activation(x_in[:, c, :], x_in[:, c, :], ACT.Identity, bias=shift_x[:, c:c + 1],
                                   scale=rstd[:, c:c + 1]).then_inc(xn_ready, 1)

            def hT_hi_of(g, k):
                act.activation(hT_hi[:, k, g * BANK:(g + 1) * BANK], xT_ps[k][:, :],
                               ACT.Relu).then_inc(hT_hi_ready, 1)

            def group_hT_hi(g):
                act.wait_ge(xT_ready, g + 1)
                for k in range(KC):
                    hT_hi_of(g, k)

            act.preload_act_table(ACT.Sqrt)
            batch_std(0)
            normalise(0, 0, ACT_CHUNKS)
            act.wait_ge(a_ps_ready, 1)
            act.activation(squares[:, :, :].rearrange("p k d -> p (k d)"), a_ps[:, :], ACT.Square,
                           accum_out=a_sumsq[:, 0:1]).then_inc(a_sumsq_ready, 1)
            act.wait_ge(xT_ready, 1)
            hT_hi_of(0, 0)
            act.wait_ge(a_total_ready, 1)
            act.activation(a_norm[:, :], max_ps[:, 0:1], ACT.Sqrt, bias=squares_floor[:, 0:1],
                           scale=OPERAND_SCALE ** -2).then_inc(a_norm_ready, 1)
            hT_hi_of(0, 1)
            act.wait_ge(inv_a_ready, 1)
            act.activation(a_hi[:, :, :].rearrange("p k d -> p (k d)"), a_ps[:, :], ACT.Copy,
                           scale=inv_a_norm[:, 0:1]).then_inc(a_hi_ready, 1)
            batch_std(1)
            act.wait_ge(wv_loaded, 16)
            act.wait_ge(a_sumsq_ready, 1)
            for k in range(KC):
                last = act.activation(squares[:, k, :], wv[:, k, :], ACT.Square, accum_out=wv_sumsq[:, k:k + 1])
            last.then_inc(wv_sumsq_ready, 1)
            act.wait_ge(wv_sumsq_ready, 1)
            act.activation(wv_norm[:, :], wv_sumsq[:, :], ACT.Sqrt, bias=squares_floor[:, 0:1],
                           scale=OPERAND_SCALE ** -2).then_inc(wv_norm_ready, 1)
            normalise(1, 0, 1)

            def split_g_hi(b):
                act.wait_ge(g_ps_ready, b + 1)
                wait_reuse(act, scores_ready, SEGS * b)
                act.activation(gT_hi[:, :, :].rearrange("p k d -> p (k d)"), g_ps[:, :], ACT.Copy
                               ).then_inc(g_hi_ready, 1)

            def take_max_row(b):
                act.wait_ge(max_row_ps_ready, b + 1)
                wait_reuse(act, shifted, GROUPS * b)
                act.activation(max_row[:, :], max_ps[:, Q:2 * Q], ACT.Copy).then_inc(max_row_ready, 1)

            def exponentials(b, par, g):
                act.wait_ge(shifted, GROUPS * b + g + 1)
                group = score[par][:, g * GC:(g + 1) * GC, :].rearrange("p c q -> p (c q)")
                act.activation(group, group, ACT.Exp, bias=log_p_scale[:, 0:1],
                               scale=a_norm[:, 0:1]).then_inc(exp_ready, 1)

            def split_p_hi(b, par, g):
                act.wait_ge(exp_ready, GROUPS * b + g + 1)
                wait_reuse(act, weighted, GROUPS * (b - 1) + g + 1)
                act.activation(p_hi[:, g * GC:(g + 1) * GC, :].rearrange("p c q -> p (c q)"),
                               score[par][:, g * GC:(g + 1) * GC, :].rearrange("p c q -> p (c q)"),
                               ACT.Copy).then_inc(hi_ready, 1)

            def v_hi_of(g):
                act.wait_ge(v_ps_ready, g + 1)
                wait_reuse(act, v_ready, g - 1)
                v_ps = seg_ps[1][:, :].rearrange("p (c d) -> p c d", d=D)
                act.activation(v_hi[:, g * XG:(g + 1) * XG, 0:D], v_ps, ACT.Copy)
                act.activation(v_f[g % 2], v_ps, ACT.Copy).then_inc(v_read, 1)

            def stage(i, par):
                is_first = isinstance(i, int) and i == 1
                if exists(i - 1):
                    take_max_row(i - 1)
                for g in range(GROUPS):
                    if g == GROUPS - 1 and is_first:
                        split_g_hi(i + 1)
                    if exists(i - 1):
                        exponentials(i - 1, 1 - par, g)
                    if g == GROUPS - 1 and exists(i + 1) and not is_first:
                        split_g_hi(i + 1)
                    if exists(i - 1):
                        split_p_hi(i - 1, 1 - par, g)

            split_g_hi(0)
            normalise(1, 1)
            act.wait_ge(wvT_ready, 1)
            act.activation(wvT_hi[:, :, :].rearrange("p k d -> p (k d)"), wvT_ps[:, 0:KC * D],
                           ACT.Copy).then_inc(wvT_hi_ready, 1)
            group_hT_hi(1)
            for g in range(XGROUPS):
                if g == 0:
                    batch_std(2)
                elif g + 1 < XGROUPS:
                    group_hT_hi(g + 1)
                if g in (2, 4):
                    batch_std(2 + g // 2)
                if g + 2 < XGROUPS:
                    normalise(g + 2)
                if g == XGROUPS - 1:
                    split_g_hi(1)
                v_hi_of(g)
            stages(act, stage)

        @block.vector
        def _(dve):
            steps = [0]

            def step(instruction):
                instruction.then_inc(dve_step, 1)
                steps[0] = steps[0] + 1
                dve.wait_ge(dve_step, steps[0])

            def group_stats(g):
                dve.wait_ge(x_loaded[g], 16)
                for c in range(g * XG, (g + 1) * XG):
                    last = dve.bn_stats(stats[:, c, :], x_in[:, c, :])
                step(last)
                for c in range(g * XG, (g + 1) * XG):
                    last = dve.bn_aggr(mean_var[:, c, :], stats[:, c, :])
                step(last)

            def batch_var(n):
                cols = slice(BATCHES[n][0] * XG, BATCHES[n][1] * XG)
                dve.tensor_scalar(var_eps[:, cols], mean_var[:, cols, 1], LN_EPS, None,
                                  ALU.add).then_inc(var_ready, 1)

            def batch_rstd(n):
                cols = slice(BATCHES[n][0] * XG, BATCHES[n][1] * XG)
                dve.wait_ge(std_ready, n + 1)
                step(dve.reciprocal(rstd0[:, cols], std[:, cols]))
                step(dve.tensor_tensor(newton[:, cols], rstd0[:, cols], rstd0[:, cols], ALU.mult))
                step(dve.tensor_tensor(newton[:, cols], newton[:, cols], var_eps[:, cols], ALU.mult))
                step(dve.tensor_scalar(newton[:, cols], newton[:, cols], -0.5, 1.5, ALU.mult, ALU.add))
                step(dve.tensor_tensor(rstd[:, cols], newton[:, cols], rstd0[:, cols], ALU.mult))
                dve.scalar_tensor_tensor(shift_x[:, cols], mean_var[:, cols, 0], -1.0, rstd[:, cols],
                                         ALU.mult, ALU.mult).then_inc(rstd_ready, 1)

            def group_hT_lo(g):
                for k in range(KC):
                    dve.wait_ge(hT_hi_ready, KC * g + k + 1)
                    cols = slice(g * BANK, (g + 1) * BANK)
                    last = dve.scalar_tensor_tensor(hT_lo[:, k, cols], xT_ps[k][:, :], 0.0, hT_hi[:, k, cols],
                                                    ALU.max, ALU.subtract)
                last.then_inc(hT_ready, 1)

            def split_g_lo(b):
                dve.wait_ge(g_hi_ready, b + 1)
                dve.tensor_tensor(gT_lo[:, :, :].rearrange("p k d -> p (k d)"), g_ps[:, :],
                                  gT_hi[:, :, :].rearrange("p k d -> p (k d)"), ALU.subtract).then_inc(g_ready, 1)

            def mask(b, par, s):
                if s == 0:
                    dve.wait_ge(edges_loaded, 16 * b + 16)
                if s % 2 == 0:
                    dve.wait_ge(filled, GROUPS * b + s // 2 + 1)
                wait_alone(dve, scores_ready, SEGS * b + s + 1)
                chunks = slice(s * SEG_CHUNKS, (s + 1) * SEG_CHUNKS)
                dve.copy_predicated(score[par][:, chunks, :].rearrange("p c q -> p (c q)"),
                                    edges[par][:, chunks, :].rearrange("p c q -> p (c q)"),
                                    segment_ps(b, s)[:, :]).then_inc(scores_masked, 1)

            def max_over_group(b, par, g):
                dve.wait_ge(scores_masked, SEGS * b + 2 * g + 2)
                step(dve.reduce_max(group_max[:, g, :],
                                    score[par][:, g * GC:(g + 1) * GC, :].rearrange("p c q -> p q c"), AX_X))

            def max_over_chunks():
                dve.reduce_max(block_max[:, :], group_max[:, :, :].rearrange("p g q -> p q g"),
                               AX_X).then_inc(block_max_ready, 1)

            def max_over_partitions(b):
                dve.wait_ge(max_turned, b + 1)
                step(dve.reduce_max(query_max[:, :], max_ps[:, 0:Q].rearrange("p (t k) -> p t k", t=QT), AX_X))
                step(dve.tensor_scalar(query_max[:, :], query_max[:, :], NO_EDGE_MAX, None, ALU.max))
                for t in range(QT):
                    last = dve.tensor_scalar(max_diag[:, t, :], ident[:, :], query_max[:, t:t + 1], None, ALU.mult)
                last.then_inc(max_diag_ready, 1)

            def split_p_lo(b, par, g):
                dve.wait_ge(hi_ready, GROUPS * b + g + 1)
                chunks = slice(g * GC, (g + 1) * GC)
                dve.tensor_tensor(p_lo[:, chunks, :], score[par][:, chunks, :], p_hi[:, chunks, :],
                                  ALU.subtract).then_inc(lo_ready, 1)

            def scale_sums(b):
                dve.wait_ge(weighted, GROUPS * (b + 1))
                for t in range(QT):
                    last = dve.tensor_scalar(sums[:, t:t + 1], sums_ps(b, t)[:, D:D + 1], 1.0, None, ALU.max)
                step(last)
                step(dve.reciprocal(inv_sums[:, :], sums[:, :]))
                wait_reuse(dve, y_ready, b)
                for t in range(QT):
                    last = dve.scalar_tensor_tensor(attn[:, t, :], sums_ps(b, t)[:, 0:D], inv_sums[:, t:t + 1],
                                                    v_scale_row[:, :], ALU.mult, ALU.mult)
                last.then_inc(attn_ready, 1)

            def finish_last(b):
                dve.wait_ge(x_res_loaded, 16 * b + 16)
                dve.wait_ge(y_stored, 16 * b)
                for t in range(QT):
                    dve.wait_ge(tile_weighted, t + 1)
                    step(dve.tensor_scalar(sums[:, t:t + 1], sums_ps(b, t)[:, D:D + 1], 1.0, None, ALU.max))
                    step(dve.reciprocal(inv_sums[:, t:t + 1], sums[:, t:t + 1]))
                    step(dve.scalar_tensor_tensor(attn[:, t, :], sums_ps(b, t)[:, 0:D], inv_sums[:, t:t + 1],
                                                  v_scale_row[:, :], ALU.mult, ALU.mult))
                    dve.tensor_tensor(y[:, t, :], attn[:, t, :], x_res[:, t, :], ALU.add).then_inc(tile_y_ready, 1)

            STAGE_STEPS = GROUPS + 2 + 2

            def stage_1():
                for g in range(GROUPS):
                    mask(1, 1, 2 * g)
                    if g == 0:
                        max_over_partitions(0)
                    mask(1, 1, 2 * g + 1)
                    if g == GROUPS - 1:
                        split_p_lo(0, 0, 1)
                        split_g_lo(2)
                    max_over_group(1, 1, g)
                    if g == GROUPS - 2:
                        split_p_lo(0, 0, 0)
                max_over_chunks()
                split_p_lo(0, 0, 2)

            def stage(i, par):
                if not isinstance(i, int) and par == 0:
                    steps[0] = loop_base[0] + (i - LOOP_FROM) * STAGE_STEPS
                for g in range(GROUPS):
                    if g == GROUPS // 2 and exists(i - 2) and not is_last(i - 2):
                        scale_sums(i - 2)
                    if exists(i):
                        mask(i, par, 2 * g)
                    if g == 0 and exists(i - 1):
                        max_over_partitions(i - 1)
                    if exists(i):
                        mask(i, par, 2 * g + 1)
                        max_over_group(i, par, g)
                    if g == GROUPS - 1:
                        if exists(i + 1):
                            split_g_lo(i + 1)
                        if exists(i):
                            max_over_chunks()
                    if g == 0 and exists(i - 2):
                        split_p_lo(i - 2, par, GROUPS - 1)
                    if g > 0 and exists(i - 1):
                        split_p_lo(i - 1, 1 - par, g - 1)
                if is_last(i - 2):
                    finish_last(i - 2)
                if isinstance(i, int) and i == LOOP_FROM - 1:
                    loop_base[0] = steps[0]

            loop_base = [0]
            group_stats(0)
            batch_var(0)
            batch_rstd(0)
            dve.wait_ge(rstd_ready, 1)
            for c in range(ACT_CHUNKS, XG):
                last = dve.tensor_scalar(x_in[:, c, :], x_in[:, c, :], rstd[:, c:c + 1], shift_x[:, c:c + 1],
                                         ALU.mult, ALU.add)
            last.then_inc(xn_rest_ready, 1)
            group_stats(1)
            batch_var(1)
            dve.wait_ge(a_norm_ready, 1)
            dve.reciprocal(inv_a_norm[:, :], a_norm[:, :]).then_inc(inv_a_ready, 1)
            group_hT_lo(0)
            dve.wait_ge(inv_a_ready, 1)
            dve.wait_ge(a_hi_ready, 1)
            dve.scalar_tensor_tensor(a_lo[:, :, :].rearrange("p k d -> p (k d)"), a_ps[:, :], inv_a_norm[:, 0:1],
                                     a_hi[:, :, :].rearrange("p k d -> p (k d)"),
                                     ALU.mult, ALU.subtract).then_inc(a_ready, 1)
            batch_rstd(1)
            dve.wait_ge(wv_norm_ready, 1)
            step(dve.reciprocal(inv_wv_norm[:, :], wv_norm[:, :]))
            for k in range(KC):
                last = dve.tensor_scalar(wv[:, k, :], wv[:, k, :], inv_wv_norm[:, k:k + 1], None, ALU.mult)
            last.then_inc(wv_scaled, 1)
            split_g_lo(0)
            group_stats(2)
            dve.wait_ge(wvT_hi_ready, 1)
            dve.tensor_tensor(wvT_lo[:, :, :].rearrange("p k d -> p (k d)"), wvT_ps[:, 0:KC * D],
                              wvT_hi[:, :, :].rearrange("p k d -> p (k d)"), ALU.subtract).then_inc(wv_ready, 1)
            group_hT_lo(1)
            group_stats(3)
            batch_var(2)
            for g in range(XGROUPS):
                if g in (0, 2, 4):
                    batch_rstd(2 + g // 2)
                if 0 < g < XGROUPS - 1:
                    group_hT_lo(g + 1)
                mask(0, 0, g)
                if g == 0:
                    dve.wait_ge(norm_row_ready, 1)
                    dve.tensor_copy(v_scale_row[:, :], max_ps[:, Q:Q + D])
                if g == XGROUPS - 1:
                    split_g_lo(1)
                if g % 2:
                    max_over_group(0, 0, g // 2)
                if g + 4 < XGROUPS:
                    group_stats(g + 4)
                    if g % 2:
                        batch_var(3 + g // 2)
            max_over_chunks()
            stage_1()
            for i in range(2, LOOP_FROM):
                stage(i, i % 2)
            with dve.Fori(LOOP_FROM, LOOP_TO, 2) as i:
                stage(i, 0)
                stage(i + 1, 1)
            steps[0] = loop_base[0] + (LOOP_TO - LOOP_FROM) * STAGE_STEPS
            for i in range(LOOP_TO, BLOCKS + 2):
                stage(i, i % 2)

        @block.tensor
        def _(pe):
            def turn_x(g):
                wait_reuse(pe, hT_ready, g)
                for c in range(XG):
                    if g == 0 and c >= ACT_CHUNKS:
                        pe.wait_ge(xn_rest_ready, 1)
                    else:
                        pe.wait_ge(xn_ready, c + 1 + (ACT_CHUNKS + (g - 1) * XG if g else 0))
                    for k in range(KC):
                        last = pe.transpose(xT_ps[k][:, c * P:(c + 1) * P],
                                            x_in[:, g * XG + c, k * P:(k + 1) * P], ident[:, :])
                last.then_inc(xT_ready, 1)

            pe.wait_ge(consts_ready, 1)
            for _ in range(WARM_UP):
                pe.matmul(seg_ps[0][:, 0:P], ones[:, :], ident[:, :], start=True, stop=True)
            pe.wait_ge(wqk_loaded, 32)
            for m in range(KC):
                for k in range(KC):
                    last = pe.matmul(a_ps[:, m * D:(m + 1) * D], wq[:, k, m * P:(m + 1) * P], wk[:, k, :],
                                     start=(k == 0), stop=(k == KC - 1))
            last.then_inc(a_ps_ready, 1)
            turn_x(0)
            pe.wait_ge(a_sumsq_ready, 1)
            pe.matmul(max_ps[:, 0:1], ones[:, :], a_sumsq[:, 0:1], start=True, stop=True).then_inc(a_total_ready, 1)

            def turn_wv():
                pe.wait_ge(wv_scaled, 1)
                for k in range(KC):
                    for m in range(KC):
                        last = pe.transpose(wvT_ps[:, m * D + k * P:m * D + (k + 1) * P],
                                            wv[:, k, m * P:(m + 1) * P], ident[:, :])
                last.then_inc(wvT_ready, 1)

            def spread_norms():
                pe.wait_ge(norm_diag_ready, 1)
                for k in range(KC):
                    last = pe.matmul(max_ps[:, Q + k * P:Q + (k + 1) * P], ones[:, :], norm_diag[:, k, :],
                                     start=True, stop=True)
                last.then_inc(norm_row_ready, 1)

            def project_g(b):
                passes = [(a, h, k) for a, h in ((a_hi, hT_hi), (a_hi, hT_lo), (a_lo, hT_hi)) for k in range(KC)]
                for m in range(KC):
                    for i, (a, h, k) in enumerate(passes):
                        last = pe.matmul(g_ps[:, m * Q:(m + 1) * Q], a[:, k, m * P:(m + 1) * P],
                                         h[:, k, bass.ds(b * Q, Q)],
                                         start=(i == 0), stop=(i == len(passes) - 1))
                last.then_inc(g_ps_ready, 1)

            def scores(b, s):
                passes = [(h, q, k) for h, q in ((hT_hi, gT_hi), (hT_hi, gT_lo), (hT_lo, gT_hi)) for k in range(KC)]
                for j in range(SEG_CHUNKS):
                    c = s * SEG_CHUNKS + j
                    for i, (h, q, k) in enumerate(passes):
                        last = pe.matmul(segment_ps(b, s)[:, j * Q:(j + 1) * Q], h[:, k, c * P:(c + 1) * P],
                                         q[:, k, :], start=(i == 0), stop=(i == len(passes) - 1))
                last.then_inc(scores_ready, 1)

            def turn_max(b):
                pe.wait_ge(block_max_ready, b + 1)
                wait_reuse(pe, max_row_ready, b)
                for t in range(QT):
                    last = pe.transpose(max_ps[:, t * P:(t + 1) * P], block_max[:, t * P:(t + 1) * P], ident[:, :])
                last.then_inc(max_turned, 1)

            def spread_max(b):
                pe.wait_ge(max_diag_ready, b + 1)
                for t in range(QT):
                    last = pe.matmul(max_ps[:, Q + t * P:Q + (t + 1) * P], ones[:, :], max_diag[:, t, :],
                                     start=True, stop=True)
                last.then_inc(max_row_ps_ready, 1)

            def project_v(g):
                wait_reuse(pe, v_read, g)
                passes = [(h, w, k) for h, w in ((hT_hi, wvT_hi), (hT_hi, wvT_lo), (hT_lo, wvT_hi)) for k in range(KC)]
                for j in range(XG):
                    c = g * XG + j
                    for i, (h, w, k) in enumerate(passes):
                        last = pe.matmul(seg_ps[1][:, j * D:(j + 1) * D], h[:, k, c * P:(c + 1) * P],
                                         w[:, k, :], start=(i == 0), stop=(i == len(passes) - 1))
                last.then_inc(v_ps_ready, 1)

            def weigh_chunk(b, c, t):
                tile = slice(t * P, (t + 1) * P)
                pe.matmul(sums_ps(b, t)[:, 0:D + 1], p_hi[:, c, tile], v_hi[:, c, 0:D + 1], start=(c == 0), stop=False)
                pe.matmul(sums_ps(b, t)[:, 0:D], p_hi[:, c, tile], v_lo[:, c, :], start=False, stop=False)
                return pe.matmul(sums_ps(b, t)[:, 0:D + 1], p_lo[:, c, tile], v_hi[:, c, 0:D + 1],
                                 start=False, stop=(c == CHUNKS - 1))

            def weigh(b, g, halfway=None):
                if g == 0 and not is_last(b):
                    wait_reuse(pe, attn_ready, b)
                if isinstance(b, int) and b == 0:
                    pe.wait_ge(v_ready, 2 * (g + 1))
                pe.wait_ge(lo_ready, GROUPS * b + g + 1)
                chunks = range(g * GC, (g + 1) * GC)
                if is_last(b) and g == GROUPS - 1:
                    for t in range(QT):
                        for c in chunks:
                            last = weigh_chunk(b, c, t)
                        last.then_inc(tile_weighted, 1)
                    return
                for c in chunks:
                    if halfway is not None and c == g * GC + GC // 2:
                        halfway()
                    for t in range(QT):
                        last = weigh_chunk(b, c, t)
                last.then_inc(weighted, 1)

            def segment(i, s):
                if isinstance(i, int) and i == 1 and s < 2:
                    pe.wait_ge(*((scores_masked, SEGS), (v_read, XGROUPS))[s])
                else:
                    pe.wait_ge(scores_masked, SEGS * i + s - 1)
                scores(i, s)

            def stage_1():
                pe.wait_ge(g_ready, 2)
                for s in range(SEGS):
                    segment(1, s)
                    if s == 1:
                        turn_max(0)
                    if s == 2:
                        spread_max(0)
                project_g(2)
                weigh(0, 0)
                weigh(0, 1)

            def stage(i, par):
                if exists(i):
                    pe.wait_ge(g_ready, i + 1)
                for g in range(GROUPS):
                    if exists(i):
                        segment(i, 2 * g)
                        segment(i, 2 * g + 1)
                    if g == 0 and exists(i - 1):
                        turn_max(i - 1)
                    if g == GROUPS - 1 and exists(i + 1):
                        project_g(i + 1)
                    if g < GROUPS // 2:
                        if exists(i - 2):
                            weigh(i - 2, g + GROUPS // 2,
                                  (lambda: spread_max(i - 1)) if g == 0 and exists(i - 1) else None)
                    elif exists(i - 1):
                        weigh(i - 1, g - GROUPS // 2)

            def stages_from_last_scores(i):
                pe.wait_ge(g_ready, i + 1)
                for g in range(GROUPS):
                    segment(i, 2 * g)
                    segment(i, 2 * g + 1)
                    if g == 0:
                        turn_max(i - 1)
                    if g < GROUPS // 2:
                        weigh(i - 2, g + GROUPS // 2, (lambda: spread_max(i - 1)) if g == 0 else None)
                weigh(i - 1, 0)
                weigh(i - 1, 1, lambda: turn_max(i))
                spread_max(i)
                weigh(i - 1, 2)
                weigh(i - 1, 3)
                for g in range(GROUPS):
                    weigh(i, g)

            pe.wait_ge(a_ready, 1)
            pe.wait_ge(hT_ready, 1)
            project_g(0)
            turn_wv()
            turn_x(1)
            spread_norms()
            pe.wait_ge(g_ready, 1)
            for g in range(XGROUPS):
                if g > 0 and g + 1 < XGROUPS:
                    turn_x(g + 1)
                pe.wait_ge(hT_ready, g + 1)
                wait_reuse(pe, scores_masked, g)
                scores(0, g)
                if g == 0:
                    pe.wait_ge(wv_ready, 1)
                if g == XGROUPS - 1:
                    project_g(1)
                project_v(g)
            stage_1()
            for i in range(2, LOOP_FROM):
                stage(i, i % 2)
            with pe.Fori(LOOP_FROM, LOOP_TO, 2) as i:
                stage(i, 0)
                stage(i + 1, 1)
            for i in range(LOOP_TO, BLOCKS - 1):
                stage(i, i % 2)
            stages_from_last_scores(BLOCKS - 1)


def kernel(x, adj, L0_gnn_Wq, L0_gnn_Wk, L0_gnn_Wv):
    import numpy as np
    import concourse.bacc as bacc
    from concourse.bass_utils import run_bass_kernel_spmd

    nc = bacc.Bacc("TRN2", target_bir_lowering=False, num_devices=1)
    arrays, args = {}, []
    for name, a in (("x", x), ("adj", adj), ("Wq", L0_gnn_Wq), ("Wk", L0_gnn_Wk), ("Wv", L0_gnn_Wv)):
        a = np.ascontiguousarray(a)
        arrays[f"in_{name}"] = a
        args.append(nc.dram_tensor(f"in_{name}", a.shape, mybir.dt.from_np(a.dtype), kind="ExternalInput").ap())
    out = nc.dram_tensor("out", arrays["in_x"].shape, F32, kind="ExternalOutput").ap()
    attention_layer(nc, *args, out)
    r = run_bass_kernel_spmd(nc, [arrays], core_ids=[0])
    return r.results[0]["out"]
```
